# Optimizing a Trainium2 kernel written in Bass

```python
import numpy as np
import jax
import jax.numpy as jnp

def _softmax(x, axis=-1):
    return jax.nn.softmax(x, axis=axis)

def _gelu(x):
    return jax.nn.gelu(x, approximate=True)

def _silu(x):
    return jax.nn.silu(x)

def _sigmoid(x):
    return jax.nn.sigmoid(x)

def _layernorm(x, axis=-1, eps=1e-05):
    m = jnp.mean(x, axis=axis, keepdims=True)
    v = jnp.var(x, axis=axis, keepdims=True)
    return (x - m) / jnp.sqrt(v + eps)

def _scatter_add(tgt, idx, src, axis=0):
    return tgt.at[idx].add(src)

def _segment_sum(src, seg, n):
    return jax.ops.segment_sum(src, seg, n)
kernel_name = 'mk_seq_postln_d1_jaxref_r4_983633'

def setup_inputs(seed: int=0):
    np.random.seed(seed)
    _w = jnp.asarray

    def _L0_attn_setup():
        import jax, jax.numpy as jnp
        import numpy as np
        NUM_HEADS = 16

        def _heads(t, B, L, nh, hd):
            return t.reshape(B, L, nh, hd).transpose(0, 2, 1, 3)

        def _attention(q, k, v, bias):
            hd = q.shape[-1]
            scores = jnp.einsum('bhqd,bhkd->bhqk', q, k) / jnp.sqrt(jnp.float32(hd))
            if bias is not None:
                scores = scores + bias[None, None]
            attn = jax.nn.softmax(scores, axis=-1)
            return jnp.einsum('bhqk,bhkd->bhqd', attn, v)
        key = jax.random.key(seed)
        ks = jax.random.split(key, 5)
        B, L, H = (4, 256, 256)
        s = 0.02
        return {'x': jax.random.normal(ks[0], (B, L, H), jnp.float32), 'Wq': jax.random.normal(ks[1], (H, H), jnp.float32) * s, 'Wkv_short': jax.random.normal(ks[2], (H, 2 * H), jnp.float32) * s, 'Wkv_long': jax.random.normal(ks[3], (H, 2 * H), jnp.float32) * s, 'Wo': jax.random.normal(ks[4], (H, H), jnp.float32) * s, 'mix_weight': jnp.float32(0.5), 'decay_factor': jnp.float32(0.95)}
    _L0_attn_in = _L0_attn_setup()

    def _L0_ffn_setup():
        import jax, jax.numpy as jnp
        import numpy as np
        from jax import lax
        T, B, I, M, O = (64, 64, 256, 256, 256)

        def _xavier(key, shape):
            fan_out, fan_in = shape
            limit = float(np.sqrt(6.0 / (fan_in + fan_out)))
            return jax.random.uniform(key, shape, jnp.float32, -limit, limit)
        key = jax.random.key(seed)
        ks = jax.random.split(key, 9)
        x = jax.random.normal(ks[0], (T, B, I), jnp.float32)
        return {'x': x, 'wf': _xavier(ks[1], (M, I)), 'uf': _xavier(ks[2], (M, M)), 'bf': jnp.zeros((M,), jnp.float32), 'wi': _xavier(ks[3], (M, I)), 'ui': _xavier(ks[4], (M, M)), 'bi': jnp.zeros((M,), jnp.float32), 'wc': _xavier(ks[5], (M, I)), 'uc': _xavier(ks[6], (M, M)), 'bc': jnp.zeros((M,), jnp.float32), 'wo': _xavier(ks[7], (O, I)), 'uo': _xavier(ks[8], (O, M)), 'bo': jnp.zeros((O,), jnp.float32), 'in_c': jnp.zeros((M,), jnp.float32)}
    _L0_ffn_in = _L0_ffn_setup()
    _d = {'L0_attn_x': _L0_attn_in['x'], 'L0_attn_Wq': _L0_attn_in['Wq'], 'L0_attn_Wkv_short': _L0_attn_in['Wkv_short'], 'L0_attn_Wkv_long': _L0_attn_in['Wkv_long'], 'L0_attn_Wo': _L0_attn_in['Wo'], 'L0_attn_mix_weight': _L0_attn_in['mix_weight'], 'L0_attn_decay_factor': _L0_attn_in['decay_factor'], 'L0_ffn_wf': _L0_ffn_in['wf'], 'L0_ffn_uf': _L0_ffn_in['uf'], 'L0_ffn_bf': _L0_ffn_in['bf'], 'L0_ffn_wi': _L0_ffn_in['wi'], 'L0_ffn_ui': _L0_ffn_in['ui'], 'L0_ffn_bi': _L0_ffn_in['bi'], 'L0_ffn_wc': _L0_ffn_in['wc'], 'L0_ffn_uc': _L0_ffn_in['uc'], 'L0_ffn_bc': _L0_ffn_in['bc'], 'L0_ffn_wo': _L0_ffn_in['wo'], 'L0_ffn_uo': _L0_ffn_in['uo'], 'L0_ffn_bo': _L0_ffn_in['bo'], 'L0_ffn_in_c': _L0_ffn_in['in_c']}
    _x0 = _d['L0_attn_x']
    _d['L0_attn_x'] = jax.random.normal(jax.random.fold_in(jax.random.key(seed), 1), (16, 512, 256), dtype=_x0.dtype)
    del _x0
    return _d

def reference(L0_attn_x, L0_attn_Wq, L0_attn_Wkv_short, L0_attn_Wkv_long, L0_attn_Wo, L0_attn_mix_weight, L0_attn_decay_factor, L0_ffn_wf, L0_ffn_uf, L0_ffn_bf, L0_ffn_wi, L0_ffn_ui, L0_ffn_bi, L0_ffn_wc, L0_ffn_uc, L0_ffn_bc, L0_ffn_wo, L0_ffn_uo, L0_ffn_bo, L0_ffn_in_c):

    def _L0_attn_ref(x, Wq, Wkv_short, Wkv_long, Wo, mix_weight, decay_factor):
        import jax, jax.numpy as jnp
        import numpy as np
        NUM_HEADS = 16

        def _heads(t, B, L, nh, hd):
            return t.reshape(B, L, nh, hd).transpose(0, 2, 1, 3)

        def _attention(q, k, v, bias):
            hd = q.shape[-1]
            scores = jnp.einsum('bhqd,bhkd->bhqk', q, k) / jnp.sqrt(jnp.float32(hd))
            if bias is not None:
                scores = scores + bias[None, None]
            attn = jax.nn.softmax(scores, axis=-1)
            return jnp.einsum('bhqk,bhkd->bhqd', attn, v)
        B, L, H = x.shape
        nh = NUM_HEADS
        hd = H // nh
        q = _heads(x @ Wq, B, L, nh, hd)
        kv_s = x @ Wkv_short
        k_s = _heads(kv_s[..., :H], B, L, nh, hd)
        v_s = _heads(kv_s[..., H:], B, L, nh, hd)
        pos = jnp.arange(L, dtype=jnp.float32)
        decay_bias = -jnp.abs(pos[None, :] - pos[:, None]) * (1.0 - decay_factor)
        out_short = _attention(q, k_s, v_s, decay_bias)
        kv_l = x @ Wkv_long
        k_l = _heads(kv_l[..., :H], B, L, nh, hd)
        v_l = _heads(kv_l[..., H:], B, L, nh, hd)
        out_long = _attention(q, k_l, v_l, None)
        alpha = jax.nn.sigmoid(mix_weight)
        out = alpha * out_short + (1.0 - alpha) * out_long
        out = out.transpose(0, 2, 1, 3).reshape(B, L, H)
        return out @ Wo

    def _L0_ffn_ref(x, wf, uf, bf, wi, ui, bi, wc, uc, bc, wo, uo, bo, in_c):
        import jax, jax.numpy as jnp
        import numpy as np
        from jax import lax
        T, B, I, M, O = (64, 64, 256, 256, 256)

        def _xavier(key, shape):
            fan_out, fan_in = shape
            limit = float(np.sqrt(6.0 / (fan_in + fan_out)))
            return jax.random.uniform(key, shape, jnp.float32, -limit, limit)
        batch = x.shape[1]
        c0 = jnp.broadcast_to(in_c, (batch, in_c.shape[0]))

        def step(c, xt):
            ft = jax.nn.sigmoid(xt @ wf.T + c @ uf.T + bf)
            it = jax.nn.sigmoid(xt @ wi.T + c @ ui.T + bi)
            gt = jnp.tanh(xt @ wc.T + c @ uc.T + bc)
            c = ft * c + it * gt
            return (c, None)
        c_final, _ = lax.scan(step, c0, x)
        h = jnp.tanh(jnp.einsum('tbi,oi->tbo', x, wo) + c_final @ uo.T + bo)
        return h
    x = L0_attn_x
    x = _layernorm(x + _L0_attn_ref(x, L0_attn_Wq, L0_attn_Wkv_short, L0_attn_Wkv_long, L0_attn_Wo, L0_attn_mix_weight, L0_attn_decay_factor), axis=-1)
    x = _layernorm(x + _L0_ffn_ref(x, L0_ffn_wf, L0_ffn_uf, L0_ffn_bf, L0_ffn_wi, L0_ffn_ui, L0_ffn_bi, L0_ffn_wc, L0_ffn_uc, L0_ffn_bc, L0_ffn_wo, L0_ffn_uo, L0_ffn_bo, L0_ffn_in_c), axis=-1)
    return x

_drawn_inputs = setup_inputs


def setup_inputs(seed=0):
    import zlib

    import numpy as np

    out = dict(_drawn_inputs(seed))
    spreads = {'L0_ffn_bf': (0.0, 0.731),
     'L0_ffn_bi': (0.0, 0.691),
     'L0_ffn_bc': (0.0, 0.1),
     'L0_ffn_bo': (0.0, 0.1),
     'L0_ffn_in_c': (0.0, 0.8)}
    factors = {'L0_attn_Wq': 8.0, 'L0_attn_Wkv_short': 7.28, 'L0_attn_Wkv_long': 8.0, 'L0_attn_Wo': 7.071}
    for name, (base, spread) in spreads.items():
        noise = np.random.default_rng([zlib.crc32(name.encode()), seed]).standard_normal(out[name].shape)
        drawn = base * np.exp(spread * noise) if base else spread * noise
        out[name] = jnp.asarray(drawn.astype(out[name].dtype))
    for name, factor in factors.items():
        out[name] = (out[name] * factor).astype(out[name].dtype)
    return out
```

```python
import concourse.bass as bass
from concourse import mybir
from concourse.alu_op_type import AluOpType as ALU
from contextlib import ExitStack

F32 = mybir.dt.float32
F32R = mybir.dt.float32r
ACT = mybir.ActivationFunctionType

B, L, H = 16, 512, 256
P = 128
NH = 16
HD = H // NH
TC = L // P
KC = H // P
GH = 4
UNITS = 2 * NH // GH
SLOTS = UNITS * TC
RING = 4
AHEAD = 8
SCALE = 0.25
EPS = 1e-5

BIAS_ROW = 3 * HD
ZERO_ROW = BIAS_ROW + 4 * TC
MAX_ROW = ZERO_ROW + 1
ROWS = MAX_ROW + 2
VW = HD + 1
VHALF = 8 * VW + HD - 1

TASKS = {0: ("v", 2, 0), 3: ("v", 3, 0), 4: ("ot", 0, -1), 7: ("ot", 1, -1), 8: ("xt", 0, 1), 11: ("xt", 1, 1),
         12: ("kq", 0, 1), 15: ("kq", 1, 1), 16: ("kq", 2, 1), 19: ("wo", 0, -1), 20: ("wo", 1, -1),
         23: ("v", 0, 1), 24: ("v", 1, 1), 27: ("kq", 3, 1), 28: ("kq", 4, 1), 31: ("kq", 5, 1),
         2: ("pvt", UNITS - 1, -1)}
TASKS |= {4 * u + 6: ("pvt", u, 0) for u in range(UNITS - 1)}
TASKS |= {4 * u - 3: ("shift", u, 0) for u in range(1, UNITS)} | {SLOTS - 3: ("shift", 0, 1)}
COUNT = {"v": 4, "ot": 2, "wo": 2, "xt": 2, "kq": 6, "pvt": UNITS, "shift": UNITS}


def exists(b):
    return not isinstance(b, int) or 0 <= b < B


def wait(eng, sem, b, per, k):
    value = b * per + k
    if isinstance(value, int) and value <= 0:
        return
    eng.wait_ge(sem, value)


def bodies(eng, body):
    body(-1)
    body(0)
    with eng.Fori(1, B - 1) as b:
        body(b)
    body(B - 1)
    body(B)


def unit_of(b, u):
    return (b, u) if u < UNITS else (b + 1, u - UNITS)


def attention_phase(nc, x, x1, Wq, Wks, Wkl, Wo, mix, decay, ident, absdiff, qrows, krows, kab):
    ctx = ExitStack()
    with ctx:
        sb = lambda n, s, d=F32: ctx.enter_context(nc.sbuf_tensor(n, s, d))
        pb = lambda n, s: ctx.enter_context(nc.psum_tensor(n, s, F32))
        sem = lambda n: ctx.enter_context(nc.semaphore(n))

        w_hi, w_lo = sb("w_hi", [P, 4, KC, H], F32R), sb("w_lo", [P, 4, KC, H], F32R)
        wv_hi, wv_lo = sb("wv_hi", [P, KC, 2, 2, P], F32R), sb("wv_lo", [P, KC, 2, 2, P], F32R)
        x_in = sb("x_in", [P, TC, H])
        x_res = sb("x_res", [P, TC, H])
        xt_h, xt_l = sb("xt_h", [P, KC, L], F32R), sb("xt_l", [P, KC, L], F32R)
        kq_h, kq_l = sb("kq_h", [P, 3, 2, L], F32R), sb("kq_l", [P, 3, 2, L], F32R)
        k_op = [sb(f"k_op{i}", [ROWS, GH, L], F32R) for i in range(RING)]
        q_op = [sb(f"q_op{i}", [ROWS, GH, L], F32R) for i in range(RING)]
        vals = sb("vals", [P, TC, 2, 2, VHALF])
        probs = sb("probs", [P, 2, GH, L])
        maxes = sb("maxes", [P, 2, TC, GH])
        shift_row = sb("shift_row", [GH, 2, L], F32R)
        pv_sb = sb("pv_sb", [P, 2, L])
        rden, rdena = sb("rden", [P, 2, TC, GH]), sb("rdena", [P, 2, TC, GH])
        o_att = [sb(f"o_att{a}", [P, TC, NH, HD]) for a in range(2)]
        o_sum = sb("o_sum", [P, TC, H])
        ot_h, ot_l = sb("ot_h", [P, KC, L], F32R), sb("ot_l", [P, KC, L], F32R)
        res = sb("res", [P, TC, H])
        stats, mv = sb("stats", [P, TC, 6]), sb("mv", [P, TC, 2])
        veps, rstd, nmr = (sb(n, [P, TC]) for n in ("veps", "rstd", "nmr"))
        consts = sb("consts", [P, 3, TC])
        id_sb, id_r = sb("id_sb", [P, P]), sb("id_r", [P, P], F32R)
        dist = sb("dist", [P, P])
        dist_h, dist_l = sb("dist_h", [P, P], F32R), sb("dist_l", [P, P], F32R)
        small = sb("small", [P, 8])
        kab_sb = sb("kab_sb", [ROWS - BIAS_ROW, 4])
        NR = ROWS - BIAS_ROW

        stage = probs[:, :, :, :].rearrange("p a h n -> p (a h n)")
        st_q = stage[:, 0:512].rearrange("p (k n) -> p k n", k=KC)
        st_kv = [stage[:, 512 + 1024 * a:1536 + 1024 * a].rearrange("p (k n) -> p k n", k=KC) for a in range(2)]
        st_o = stage[:, 2560:3072].rearrange("p (k n) -> p k n", k=KC)
        rows_in = o_sum[:, :, :].rearrange("p t n -> p (t n)")
        rows_tmp = res[:, :, :].rearrange("p t n -> p (t n)")
        rows_out = ot_h[:, :, :].rearrange("p k n -> p (k n)")
        rows_h = ot_l[:, :, :].rearrange("p k n -> p (k n)")

        b_ps = [pb(f"b_ps{i}", [P, 2, L]) for i in range(2)]
        a_ps = [pb(f"a_ps{i}", [P, L]) for i in range(2)]
        pv_ps = pb("pv_ps", [P, L])
        work = pb("work", [P, L])

        const_in, rows_set, setup, ones_set, exp_mix = map(sem, ("const_in", "rows_set", "setup", "ones_set", "exp_mix"))
        x_loaded, res_loaded, x1_stored = map(sem, ("x_loaded", "res_loaded", "x1_stored"))
        k_loaded = [sem(f"k_loaded{i}") for i in range(RING)]
        q_loaded = [sem(f"q_loaded{i}") for i in range(RING)]
        shift_loaded = [sem(f"shift_loaded{i}") for i in range(2)]
        full = {n: sem(f"{n}_full") for n in COUNT}
        b_full, a_full, pv_full = map(sem, ("b_full", "a_full", "pv_full"))
        a_reduced, exp_done, pv_copied = map(sem, ("a_reduced", "exp_done", "pv_copied"))
        xt_hi, kq_hi, ot_hi = map(sem, ("xt_hi", "kq_hi", "ot_hi"))
        rden_done, rdena_done, osum_done, bn_done, mv_done = map(sem, ("rden_done", "rdena_done", "osum_done", "bn_done", "mv_done"))
        ln_step, normed = map(sem, ("ln_step", "normed"))
        done = {n: sem(f"{n}_done") for n in COUNT}
        N_SETUP = 30

        block = ctx.enter_context(nc.Block())

        @block.sync
        def _(sp):
            copy_words = lambda dst, src: sp.dma_start(dst.bitcast(F32), src.bitcast(F32))
            for dst, src in ((st_q, Wq.rearrange("(k p) n -> p k n", p=P)), (st_kv[0], Wkl.rearrange("(k p) n -> p k n", p=P)),
                             (st_kv[1], Wks.rearrange("(k p) n -> p k n", p=P)), (st_o, Wo.rearrange("(k p) n -> p k n", p=P)),
                             (id_sb[:, :], ident), (dist[:, :], absdiff),
                             (rows_in[0:NR, 0:L], krows), (rows_tmp[0:NR, 0:2 * L], qrows), (kab_sb[:, :], kab),
                             (small[:, 0:1], mix.unsqueeze(0).to_broadcast([P, 1])), (small[:, 1:2], decay.unsqueeze(0).to_broadcast([P, 1]))):
                sp.dma_start(dst, src).then_inc(const_in, 16)
            sp.wait_ge(setup, N_SETUP)
            for h in range(GH):
                for i in range(RING):
                    copy_words(q_op[i][BIAS_ROW:MAX_ROW, h, :], rows_h[0:NR - 2, 0:L]).then_inc(rows_set, 16)
                for i in range(RING):
                    copy_words(k_op[i][BIAS_ROW:ROWS, h, :], rows_out[0:NR, (1 - i % 2) * L:(2 - i % 2) * L]).then_inc(rows_set, 16)

            def load_rows(dst, h, part, half, pos, order, s):
                at = pos + HD * h
                for r, src in enumerate(order):
                    copy_words(dst[HD * r:HD * r + HD, h, :], src[at:at + HD, part, half, :]).then_inc(s, 16)

            def projected(b, n):
                if isinstance(b, int):
                    wait(sp, done["kq"], b, 6, n)

            def load_k(b, u, h):
                if exists(b):
                    g, att = u // 2, u % 2
                    if h == 0:
                        projected(b, 3 * (g // 2) + 2 * att + 1)
                        wait(sp, b_full, b, 2 * SLOTS, 8 * (u - RING + 1))
                    load_rows(k_op[u % RING], h, 2 * att, g // 2, 64 * (g % 2), (kq_h, kq_l, kq_h), k_loaded[u % RING])

            def load_q(b, g, h):
                if exists(b):
                    if h == 0:
                        projected(b, 3 * (g // 2) + 2)
                        wait(sp, b_full, b, 2 * SLOTS, 2 * (8 * g - 14))
                    load_rows(q_op[g], h, 1, g // 2, 64 * (g % 2), (kq_h, kq_h, kq_l), q_loaded[g])

            def body(b):
                for s in range(SLOTS):
                    if s % 4 == 0:
                        for h in range(GH):
                            load_k(*unit_of(b, s // 4 + 3), h)
                    if s % 8 == 2:
                        bb, u = unit_of(b, (s + 14) // 4)
                        for h in range(GH):
                            load_q(bb, u // 2, h)
                    if s in TASKS and TASKS[s][0] == "shift":
                        _, u, off = TASKS[s]
                        bb = b + off
                        if exists(bb):
                            wait(sp, done["shift"], bb, UNITS, u + 1)
                            for h in range(GH):
                                copy_words(q_op[u // 2][MAX_ROW + u % 2:MAX_ROW + u % 2 + 1, h, :],
                                           shift_row[h:h + 1, u % 2, :]).then_inc(shift_loaded[u % 2], 16)

            bodies(sp, body)

        @block.gpsimd
        def _(pool):
            for n, value in ((0, EPS), (1, -0.5), (2, -1.0)):
                pool.memset(consts[:, n, :], value).then_inc(ln_step, 1)
            pool.wait_ge(ln_step, 3)
            pool.memset(nmr[:, :], 0.0).then_inc(x1_stored, 16)

            def body(b):
                bb = b - 1
                if exists(bb):
                    wait(pool, done["pvt"], bb, UNITS, UNITS)
                    pool.tensor_tensor(o_sum[:, :, :], o_att[0][:, :, :, :].rearrange("p t h d -> p t (h d)"),
                                       o_att[1][:, :, :, :].rearrange("p t h d -> p t (h d)"), ALU.add).then_inc(osum_done, 1)
                    wait(pool, mv_done, bb, TC, TC)
                    pool.tensor_tensor(veps[:, :], mv[:, :, 1], consts[:, 0, :], ALU.add).then_inc(ln_step, 1)
                    wait(pool, ln_step, bb, 4, 3 + 1)
                    pool.tensor_tensor(rstd[:, :], veps[:, :], consts[:, 1, :], ALU.pow).then_inc(ln_step, 1)
                    pool.tensor_tensor(nmr[:, :], mv[:, :, 0], consts[:, 2, :], ALU.mult).then_inc(ln_step, 1)
                    wait(pool, ln_step, bb, 4, 3 + 3)
                    pool.tensor_tensor(nmr[:, :], nmr[:, :], rstd[:, :], ALU.mult).then_inc(ln_step, 1)

            bodies(pool, body)

        @block.scalar
        def _(act):
            act.wait_ge(const_in, 11 * 16)
            act.activation(small[:, 2:3], small[:, 0:1], ACT.Exp, scale=-1.0).then_inc(exp_mix, 1)

            def exp_pair(b, s, hp):
                wait(act, b_full, b, 2 * SLOTS, 2 * s + hp + 1)
                wait(act, pv_full, b, SLOTS, s - 1)
                act.activation(probs[:, s % 2, 2 * hp:2 * hp + 2, :], b_ps[hp][:, :, :], ACT.Exp).then_inc(exp_done, 1)

            def body(b):
                for s in range(SLOTS):
                    if s == 1 and exists(b + 1):
                        act.dma_start(x_in[:, :, :], x[b + 1].rearrange("(t p) n -> p t n", p=P)).then_inc(x_loaded, 16)
                    if s == 21 and exists(b):
                        wait(act, done["wo"], b, 2, 0)
                        act.dma_start(x_res[:, :, :], x[b].rearrange("(t p) n -> p t n", p=P)).then_inc(res_loaded, 16)
                    if s == 25 and exists(b - 1):
                        wait(act, ln_step, b - 1, 4, 3 + 4)
                        for t in range(TC):
                            act.activation(res[:, t, :], res[:, t, :], ACT.Identity, bias=nmr[:, t:t + 1],
                                           scale=rstd[:, t:t + 1]).then_inc(normed, 1)
                        wait(act, normed, b - 1, TC, TC)
                        act.dma_start(x1[b - 1].rearrange("(t p) n -> p t n", p=P), res[:, :, :]).then_inc(x1_stored, 16)
                    if exists(b):
                        exp_pair(b, s, 0)
                        exp_pair(b, s, 1)
                    if s not in TASKS or not exists(b + TASKS[s][2]):
                        continue
                    kind, n, off = TASKS[s]
                    bb = b + off
                    if kind in ("xt", "kq", "ot"):
                        dst, ready, scale = {"xt": (xt_h[:, n % 2, :], xt_hi, 1.0), "ot": (ot_h[:, n % 2, :], ot_hi, 1.0),
                                             "kq": (kq_h[:, n % 3, n // 3, :], kq_hi, SCALE if n % 3 == 1 else 1.0)}[kind]
                        wait(act, full[kind], bb, COUNT[kind], n + 1)
                        act.activation(dst, work[:, :], ACT.Copy, scale=scale).then_inc(ready, 1)
                    if kind == "v":
                        wait(act, full["v"], bb, 4, n + 1)
                        if n == 2:
                            wait(act, pv_full, bb, SLOTS, 0)
                        for j in range(2):
                            src = work[:, 256 * j:256 * j + 256].rearrange("p (a h d) -> p a h d", a=2, d=HD)
                            dst = vals[:, 2 * (n % 2) + j, n // 2, :, 0:8 * VW].rearrange("p a (h e) -> p a h e", e=VW)[:, :, :, 0:HD]
                            act.activation(dst, src, ACT.Copy).then_inc(done["v"], 1)

            bodies(act, body)
            act.wait_ge(x1_stored, 16 * B)

        @block.vector
        def _(dve):
            step = [0]

            def chain(instruction):
                step[0] += 1
                instruction.then_inc(setup, 1)
                dve.wait_ge(setup, step[0])

            def split(hi, lo, value, factor=1.0):
                chain(dve.tensor_scalar(hi, value, factor, None, ALU.mult))
                chain(dve.scalar_tensor_tensor(lo, value, factor, hi.bitcast(F32), ALU.mult, ALU.subtract))

            dve.memset(vals[:, :, :, :, :], 1.0).then_inc(ones_set, 1)
            dve.wait_ge(const_in, 11 * 16)
            split(w_hi[:, 0, :, :], w_lo[:, 0, :, :], st_q)
            for a in range(2):
                split(w_hi[:, 1 + a, :, :], w_lo[:, 1 + a, :, :], st_kv[a][:, :, 0:H])
                for k in range(KC):
                    split(wv_hi[:, k, :, a, :], wv_lo[:, k, :, a, :], st_kv[a][:, k, H:2 * H].rearrange("p (f n) -> p f n", f=2))
            split(w_hi[:, 3, :, :], w_lo[:, 3, :, :], st_o)
            dve.wait_ge(exp_mix, 1)
            chain(dve.tensor_scalar(small[:, 3:4], small[:, 2:3], 1.0, None, ALU.add))
            chain(dve.reciprocal(small[:, 5:6], small[:, 3:4]))
            chain(dve.tensor_scalar(small[:, 4:5], small[:, 5:6], -1.0, 1.0, ALU.mult, ALU.add))
            chain(dve.tensor_scalar(small[:, 6:7], small[:, 1:2], -1.0, 1.0, ALU.mult, ALU.add))
            chain(dve.tensor_scalar(dist[:, :], dist[:, :], small[:, 6:7], -1.0, ALU.mult, ALU.mult))
            split(dist_h[:, :], dist_l[:, :], dist[:, :])
            chain(dve.tensor_scalar(kab_sb[:, 3:4], kab_sb[:, 0:1], small[0:NR, 6:7], kab_sb[:, 1:2], ALU.mult, ALU.add))
            chain(dve.tensor_scalar(rows_in[0:NR, L:2 * L], rows_in[0:NR, 0:L], kab_sb[:, 3:4], None, ALU.mult))
            chain(dve.tensor_copy(id_r[:, :], id_sb[:, :]))
            chain(dve.tensor_copy(rows_h[0:NR, L:2 * L], rows_in[0:NR, L:2 * L]))
            chain(dve.scalar_tensor_tensor(rows_out[0:NR, 0:L], rows_h[0:NR, L:2 * L].bitcast(F32), kab_sb[:, 2:3],
                                           rows_in[0:NR, L:2 * L], ALU.mult, ALU.add))
            chain(dve.tensor_copy(rows_out[0:NR, L:2 * L], rows_tmp[0:NR, L:2 * L]))
            chain(dve.tensor_copy(rows_h[0:NR, 0:L], rows_tmp[0:NR, 0:L]))
            assert step[0] == N_SETUP, step[0]

            def rest(dst, hi, sem_hi, kind, bb, n, scale):
                wait(dve, sem_hi, bb, COUNT[kind], n + 1)
                dve.scalar_tensor_tensor(dst, work[:, :], scale, hi.bitcast(F32), ALU.mult, ALU.subtract).then_inc(done[kind], 1)

            def body(b):
                for s in range(SLOTS):
                    if s == 22 and exists(b - 1):
                        wait(dve, bn_done, b - 1, TC, TC)
                    bb, u = unit_of(b, (s + AHEAD) // 4)
                    def reduce(h, bb=bb, u=u, s=s):
                        if exists(bb):
                            wait(dve, a_full, bb, 16 * UNITS, 16 * u + 4 * (s % 4) + h + 1)
                            dve.reduce_max(maxes[:, u % 2, s % 4, h:h + 1], a_ps[h % 2][:, :],
                                           mybir.AxisListType.X).then_inc(a_reduced, 1)

                    by_scalar = s in TASKS and TASKS[s][0] in ("xt", "kq", "ot")
                    for h in range(3 if by_scalar else 2):
                        reduce(h)
                    if s in TASKS and exists(b + TASKS[s][2]):
                        kind, n, off = TASKS[s]
                        bb = b + off
                        if kind == "xt":
                            rest(xt_l[:, n, :], xt_h[:, n, :], xt_hi, kind, bb, n, 1.0)
                        if kind == "kq":
                            rest(kq_l[:, n % 3, n // 3, :], kq_h[:, n % 3, n // 3, :], kq_hi, kind, bb, n, SCALE if n % 3 == 1 else 1.0)
                        if kind == "ot":
                            rest(ot_l[:, n, :], ot_h[:, n, :], ot_hi, kind, bb, n, 1.0)
                        if kind == "shift":
                            wait(dve, full["shift"], bb, UNITS, n + 1)
                            wait(dve, shift_loaded[n % 2], bb, 64 * UNITS // 2, 64 * (n // 2))
                            dve.tensor_scalar(shift_row[:, n % 2, :], work[0:GH, :], -1.0, None, ALU.mult).then_inc(done["shift"], 1)
                        if kind == "pvt":
                            g, att = n // 2, n % 2
                            o = work[:, :].rearrange("p (t h e) -> p t h e", t=TC, h=GH)
                            wait(dve, full["pvt"], bb, UNITS, n + 1)
                            dve.reciprocal(rden[:, att, :, :], o[:, :, :, HD]).then_inc(rden_done, 1)
                            wait(dve, rden_done, bb, UNITS, n + 1)
                            dve.tensor_scalar(rdena[:, att, :, :], rden[:, att, :, :], small[:, 4 + att:5 + att], None,
                                              ALU.mult).then_inc(rdena_done, 1)
                            wait(dve, rdena_done, bb, UNITS, n + 1)
                            if n < 2:
                                wait(dve, osum_done, bb, 1, 0)
                            dve.tensor_tensor(o_att[att][:, :, GH * g:GH * g + GH, :], o[:, :, :, 0:HD],
                                              rdena[:, att, :, :].unsqueeze(3).to_broadcast([P, TC, GH, HD]),
                                              ALU.mult).then_inc(done["pvt"], 1)
                        if kind == "wo":
                            wait(dve, full["wo"], bb, 2, n + 1)
                            wait(dve, res_loaded, bb, 16, 16)
                            wait(dve, x1_stored, bb, 16, 16)
                            r = res[:, 2 * n:2 * n + 2, :]
                            dve.tensor_tensor(r, work[:, :].rearrange("p (t n) -> p t n", t=2), x_res[:, 2 * n:2 * n + 2, :],
                                              ALU.add).then_inc(done["wo"], 1)
                            wait(dve, done["wo"], bb, 2, n + 1)
                            for j in range(2):
                                dve.bn_stats(stats[:, 2 * n + j, :], res[:, 2 * n + j, :]).then_inc(bn_done, 1)
                    for h in range(3 if by_scalar else 2, GH):
                        reduce(h)
                    if s == 22 and exists(b - 1):
                        for t in range(TC):
                            dve.bn_aggr(mv[:, t, :], stats[:, t, :]).then_inc(mv_done, 1)
                    if s % 4 == 0:
                        bb, u = (b, s // 4 - 1) if s else (b - 1, UNITS - 1)
                        if exists(bb):
                            wait(dve, pv_full, bb, SLOTS, 4 * u + 4)
                            dve.tensor_copy(pv_sb[:, u % 2, :], pv_ps[:, :]).then_inc(pv_copied, 1)

            bodies(dve, body)

        @block.tensor
        def _(pe):
            pe.wait_ge(ones_set, 1)
            pe.wait_ge(setup, N_SETUP)
            pe.wait_ge(rows_set, 16 * GH * 2 * RING)

            def three(out, lhs, rhs):
                last = None
                pairs = [(k, a, c) for k in range(KC) for a, c in ((0, 0), (1, 0), (0, 1))]
                for i, (k, a, c) in enumerate(pairs):
                    last = pe.matmul(out, lhs(a, k), rhs(c, k), start=(i == 0), stop=(i == len(pairs) - 1))
                return last

            def score(out, lhs, rhs, chunk, rows, diagonals):
                last = pe.matmul(out, lhs[0:rows, P * chunk:P * chunk + P], rhs[0:rows, :], start=True, stop=not diagonals)
                for i, d in enumerate(diagonals):
                    last = pe.matmul(out[:, P * chunk:P * chunk + P], id_r[:, :], d[:, :], start=False, stop=(i == len(diagonals) - 1))
                return last

            def score_pair(b, s, hp):
                u, c = s // 4, s % 4
                q, k = q_op[u // 2], k_op[u % RING]
                if c == 0 and hp == 0:
                    wait(pe, shift_loaded[u % 2], b, 64 * UNITS // 2, 64 * (u // 2 + 1))
                wait(pe, exp_done, b, 2 * SLOTS, 2 * s + hp - 1)
                for j in range(2):
                    h = 2 * hp + j
                    last = score(b_ps[hp][:, j, :], k[:, h, :], q[:, h, :], c, ROWS - 1 + u % 2, (dist_h, dist_l) if u % 2 else ())
                last.then_inc(b_full, 1)

            def score_for_max(b, s, h):
                bb, u = unit_of(b, (s + AHEAD) // 4)
                c = s % 4
                if not exists(bb):
                    return
                q, k = q_op[u // 2], k_op[u % RING]
                if c == 0 and h == 0:
                    wait(pe, k_loaded[u % RING], bb, 384, 192 * (u // RING + 1))
                    wait(pe, q_loaded[u // 2], bb, 192, 192)
                wait(pe, a_reduced, bb, 16 * UNITS, 16 * u + 4 * c + h - 1)
                score(a_ps[h % 2][:, :], q[:, h, :], k[:, h, :], c, MAX_ROW, (dist_h,) if u % 2 else ()).then_inc(a_full, 1)

            def weigh(b, s):
                u, c = s // 4, s % 4
                g, att = u // 2, u % 2
                wait(pe, exp_done, b, 2 * SLOTS, 2 * s + 2)
                if c == 0:
                    wait(pe, pv_copied, b, UNITS, u)
                    if u in (0, UNITS // 2):
                        wait(pe, done["v"], b, 8, 4 if u == 0 else 8)
                for h in range(GH):
                    at = VW * (GH * (g % 2) + h)
                    last = pe.matmul(pv_ps[32 * h:32 * h + 32, :], vals[:, c, g // 2, att, at:at + 32], probs[:, s % 2, h, :],
                                     start=(c == 0), stop=(c == TC - 1))
                last.then_inc(pv_full, 1)

            def work_task(b, s):
                kind, n, off = TASKS[s]
                bb = b + off
                if not exists(bb):
                    return
                for back in range(1, SLOTS + 1):
                    at, ob = (s - back, b) if s >= back else (s - back + SLOTS, b - 1)
                    if isinstance(ob, int) and ob < -1:
                        break
                    if at in TASKS and exists(ob + TASKS[at][2]):
                        k0, n0, off0 = TASKS[at]
                        per, m = (8, 2 * n0 + 2) if k0 == "v" else (COUNT[k0], n0 + 1)
                        wait(pe, done[k0], ob + off0, per, m)
                        break
                if kind == "xt":
                    wait(pe, x_loaded, bb, 16, 16)
                    for t in range(TC):
                        last = pe.transpose(work[:, P * t:P * t + P], x_in[:, t, P * n:P * n + P], id_sb[:, :])
                if kind == "kq":
                    w, half = (1, 0, 2)[n % 3], n // 3
                    wait(pe, done["xt"], bb, 2, 2)
                    last = three(work[:, :], lambda a, k: (w_hi, w_lo)[a][:, w, k, P * half:P * half + P],
                                 lambda a, k: (xt_h, xt_l)[a][:, k, :])
                if kind == "v":
                    wait(pe, done["xt"], bb, 2, 2)
                    for j in range(2):
                        t = 2 * (n % 2) + j
                        last = three(work[:, 256 * j:256 * j + 256], lambda a, k: (xt_h, xt_l)[a][:, k, P * t:P * t + P],
                                     lambda a, k: (wv_hi, wv_lo)[a][:, k, n // 2, :, :])
                if kind == "ot":
                    wait(pe, osum_done, bb, 1, 1)
                    for t in range(TC):
                        last = pe.transpose(work[:, P * t:P * t + P], o_sum[:, t, P * n:P * n + P], id_sb[:, :])
                if kind == "wo":
                    wait(pe, done["ot"], bb, 2, 2)
                    for j in range(2):
                        t = 2 * n + j
                        last = three(work[:, 256 * j:256 * j + 256], lambda a, k: (ot_h, ot_l)[a][:, k, P * t:P * t + P],
                                     lambda a, k: (w_hi, w_lo)[a][:, 3, k, :])
                if kind == "pvt":
                    wait(pe, pv_copied, bb, UNITS, n + 1)
                    for t in range(TC):
                        last = pe.transpose(work[:, P * t:P * t + P], pv_sb[:, n % 2, P * t:P * t + P], id_sb[:, :])
                if kind == "shift":
                    wait(pe, a_reduced, bb, 16 * UNITS, 16 * n + 16)
                    for t in range(TC):
                        last = pe.transpose(work[0:GH, P * t:P * t + P], maxes[:, n % 2, t, :], id_sb[:, :])
                last.then_inc(full[kind], 1)

            def body(b):
                for s in range(SLOTS):
                    if exists(b):
                        score_pair(b, s, 0)
                    score_for_max(b, s, 0)
                    if exists(b):
                        score_pair(b, s, 1)
                    score_for_max(b, s, 1)
                    if s in TASKS:
                        work_task(b, s)
                    score_for_max(b, s, 2)
                    bb, ss = (b, s - 1) if s else (b - 1, SLOTS - 1)
                    if exists(bb):
                        weigh(bb, ss)
                    score_for_max(b, s, 3)

            bodies(pe, body)


GATES = 3


def recurrence_phase(nc, x1, wx, uc, gate_bias, wo, uo, bo, in_c, ident, out):
    T = B
    ctx = ExitStack()
    with ctx:
        sb = lambda n, s, d=F32: ctx.enter_context(nc.sbuf_tensor(n, s, d))
        pb = lambda n, s: ctx.enter_context(nc.psum_tensor(n, s, F32))
        sem = lambda n: ctx.enter_context(nc.semaphore(n))

        wx_h, wx_l = sb("wx_h", [P, GATES, KC, H], F32R), sb("wx_l", [P, GATES, KC, H], F32R)
        uc_h, uc_l = sb("uc_h", [P, GATES, KC, H], F32R), sb("uc_l", [P, GATES, KC, H], F32R)
        wo_h, wo_l = sb("wo_h", [P, 2, KC, H], F32R), sb("wo_l", [P, 2, KC, H], F32R)
        hpre = sb("hpre", [P, T, TC, H])
        x_step = sb("x_step", [P, TC, H])
        xt_h, xt_l = sb("xs_h", [P, KC, L], F32R), sb("xs_l", [P, KC, L], F32R)
        act_out = sb("act_out", [P, KC, GATES, L])
        state, keep, gain = sb("state", [P, KC, L]), sb("keep", [P, KC, L]), sb("gain", [P, KC, L])
        s_h, s_l = sb("s_h", [P, KC, L], F32R), sb("s_l", [P, KC, L], F32R)
        bias_in, bias = sb("bias_in", [P, GATES, KC]), sb("bias", [P, GATES, KC])
        c_in = sb("c_in", [P, KC])
        bo_row, c_out = sb("bo_row", [P, H]), sb("c_out", [P, TC, H])
        id_sb = sb("id2_sb", [P, P])
        x_back = sb("x_back", [P, 2, TC, H])
        summed = sb("summed", [P, 2, TC, H])
        stats, mv = sb("stats2", [P, 2, TC, 6]), sb("mv2", [P, 2, TC, 2])
        veps, rstd, nmr = (sb(n, [P, 2, TC]) for n in ("veps2", "rstd2", "nmr2"))
        consts, fence = sb("consts2", [P, 3, TC]), sb("fence", [P, 1])

        gate_ps = [pb(f"gate_ps{i}", [P, L]) for i in range(GATES * KC)]
        work = [pb(f"work2_{i}", [P, L]) for i in range(2)]

        stage = hpre[:, :, :, :].rearrange("p t c n -> p (t c n)")
        st_w = stage[:, 0:1536].rearrange("p (g k n) -> p g k n", g=GATES, k=KC)
        st_u = stage[:, 1536:3072].rearrange("p (g k n) -> p g k n", g=GATES, k=KC)
        st_o = stage[:, 3072:4096].rearrange("p (g k n) -> p g k n", g=2, k=KC)

        params_in, x_in, setup, xs_full, xs_hi, xs_lo = map(sem, ("params_in", "x_step_in", "setup2", "xs_full", "xs_hi", "xs_lo"))
        hp_full, hp_done, gate_full, gate_done, kept, gained, s_done, s_hi, s_lo = map(sem, (
            "hp_full", "hp_done", "gate_full", "gate_done", "kept", "gained", "s_done", "s_hi_done", "s_lo_done"))
        co_full, co_done, back_in, pre_done, tanh_done, sum_done, bn_done, mv_done, ln_step, normed, stored = map(sem, (
            "co_full", "co_done", "back_in", "pre_done", "tanh_done", "sum_done", "bn2_done", "mv2_done", "ln2_step", "normed2", "stored"))
        in_back = [sem(f"in_back{i}") for i in range(2)]
        out_sem = [sem(f"out_stored{i}") for i in range(2)]
        N_SETUP = 14

        block = ctx.enter_context(nc.Block())
        tokens = lambda ap: ap.rearrange("(c p) n -> p c n", p=P)

        @block.sync
        def _(sp):
            for g in range(GATES):
                sp.dma_start(st_w[:, g, :, :], wx[g].rearrange("(k p) n -> p k n", p=P)).then_inc(params_in, 16)
                sp.dma_start(st_u[:, g, :, :], uc[g].rearrange("(k p) n -> p k n", p=P)).then_inc(params_in, 16)
            for g, w in enumerate((wo, uo)):
                sp.dma_start(st_o[:, g, :, :], w.rearrange("(k p) n -> p k n", p=P)).then_inc(params_in, 16)
            sp.dma_start(bias_in[:, :, :], gate_bias).then_inc(params_in, 16)
            sp.dma_start(c_in[:, :], in_c).then_inc(params_in, 16)
            sp.dma_start(bo_row[:, :], bo.unsqueeze(0).to_broadcast([P, H])).then_inc(params_in, 16)
            sp.dma_start(id_sb[:, :], ident).then_inc(params_in, 16)
            sp.dma_start(x_step[:, :, :], tokens(x1[0])).then_inc(x_in, 16)
            for i in range(2):
                sp.dma_start(x_back[:, i, :, :], tokens(x1[i])).then_inc(in_back[i], 16)

        @block.gpsimd
        def _(pool):
            for n, value in ((0, EPS), (1, -0.5), (2, -1.0)):
                pool.memset(consts[:, n, :], value).then_inc(ln_step, 1)
            pool.wait_ge(ln_step, 3)
            pool.wait_ge(co_done, 3)
            pool.wait_ge(hp_done, 2 * T)

            def add_state(t):
                pool.tensor_tensor(hpre[:, t, :, :], hpre[:, t, :, :], c_out[:, :, :], ALU.add).then_inc(pre_done, 1)

            def scales(t2, i):
                base = t2 * 8 + 4 * i + 3
                if not isinstance(t2, int) or t2 + i > 0:
                    pool.wait_ge(normed, t2 * (2 * TC) + TC * i)
                pool.wait_ge(mv_done, t2 * (2 * TC) + TC * (i + 1))
                pool.tensor_tensor(veps[:, i, :], mv[:, i, :, 1], consts[:, 0, :], ALU.add).then_inc(ln_step, 1)
                pool.wait_ge(ln_step, base + 1)
                pool.tensor_tensor(rstd[:, i, :], veps[:, i, :], consts[:, 1, :], ALU.pow).then_inc(ln_step, 1)
                pool.tensor_tensor(nmr[:, i, :], mv[:, i, :, 0], consts[:, 2, :], ALU.mult).then_inc(ln_step, 1)
                pool.wait_ge(ln_step, base + 3)
                pool.tensor_tensor(nmr[:, i, :], nmr[:, i, :], rstd[:, i, :], ALU.mult).then_inc(ln_step, 1)

            add_state(0)
            add_state(1)
            for i in range(2):
                add_state(2 + i)
                scales(0, i)
            with pool.Fori(1, T // 2 - 1) as t2:
                for i in range(2):
                    add_state(t2 * 2 + 2 + i)
                    scales(t2, i)
            for i in range(2):
                scales(T // 2 - 1, i)

        @block.scalar
        def _(act):
            act.wait_ge(setup, N_SETUP)

            def gate(t, n):
                k, g = n // GATES, n % GATES
                act.wait_ge(gate_full, t * 6 + n + 1)
                act.activation(act_out[:, k, g, :], gate_ps[n][:, :], ACT.Tanh, bias=bias[:, g, k:k + 1],
                               scale=0.5 if g < 2 else 1.0).then_inc(gate_done, 1)

            def state_hi(t, k):
                act.wait_ge(s_done, t * 2 + k + 1)
                act.activation(s_h[:, k, :], state[:, k, :], ACT.Copy).then_inc(s_hi, 1)

            def step_hi(t, k):
                act.wait_ge(xs_full, t * 2 + k + 1)
                act.activation(xt_h[:, k, :], work[k][:, :], ACT.Copy).then_inc(xs_hi, 1)

            def keep_hpre(t):
                act.wait_ge(hp_full, t * 2 + 1)
                act.activation(hpre[:, t, 0:2, :], work[0][:, :].rearrange("p (c n) -> p c n", c=2), ACT.Copy).then_inc(hp_done, 1)

            step_hi(0, 0)
            step_hi(0, 1)
            act.dma_start(x_step[:, :, :], tokens(x1[1])).then_inc(x_in, 16)
            keep_hpre(0)

            def load_step(t):
                act.dma_start(x_step[:, :, :], tokens(x1[t])).then_inc(x_in, 16)

            def step(t, more, load):
                for n in range(5):
                    gate(t, n)
                state_hi(t, 0)
                gate(t, 5)
                if more:
                    step_hi(t + 1, 0)
                    step_hi(t + 1, 1)
                if load:
                    load_step(t + 2)
                state_hi(t, 1)
                if more:
                    keep_hpre(t + 1)

            with act.Fori(0, T - 2) as t:
                step(t, True, True)
            step(T - 2, True, False)
            step(T - 1, False, False)

            def tanh_out(t):
                act.wait_ge(pre_done, t + 1)
                act.activation(hpre[:, t, :, :], hpre[:, t, :, :], ACT.Tanh).then_inc(tanh_done, 1)

            def normalise(t2, i):
                act.wait_ge(ln_step, t2 * 8 + 4 * i + 3 + 4)
                for c in range(TC):
                    act.activation(summed[:, i, c, :], summed[:, i, c, :], ACT.Identity, bias=nmr[:, i, c:c + 1],
                                   scale=rstd[:, i, c:c + 1]).then_inc(normed, 1)
                act.wait_ge(normed, t2 * (2 * TC) + TC * (i + 1))
                act.dma_start(tokens(out[t2 * 2 + i]), summed[:, i, :, :]).then_inc(out_sem[i], 16)

            def back(t2, i):
                act.wait_ge(sum_done, t2 * 2 + i - 1)
                act.dma_start(x_back[:, i, :, :], tokens(x1[t2 * 2 + i])).then_inc(in_back[i], 16)

            tanh_out(0)
            with act.Fori(0, T // 2 - 1) as t2:
                for i in range(2):
                    tanh_out(t2 * 2 + 1 + i)
                    normalise(t2, i)
                    back(t2 + 1, i)
            tanh_out(T - 1)
            for i in range(2):
                normalise(T // 2 - 1, i)
            for i in range(2):
                act.wait_ge(out_sem[i], 16 * T // 2)

        @block.vector
        def _(dve):
            count = [0]

            def chain(instruction):
                count[0] += 1
                instruction.then_inc(setup, 1)
                dve.wait_ge(setup, count[0])

            def split(hi, lo, value, factor=1.0):
                chain(dve.tensor_scalar(hi, value, factor, None, ALU.mult))
                chain(dve.scalar_tensor_tensor(lo, value, factor, hi.bitcast(F32), ALU.mult, ALU.subtract))

            dve.wait_ge(params_in, 16 * (2 * GATES + 6))
            split(wx_h[:, :, :, :], wx_l[:, :, :, :], st_w)
            split(uc_h[:, :, :, :], uc_l[:, :, :, :], st_u, 0.5)
            split(wo_h[:, 0, :, :], wo_l[:, 0, :, :], st_o[:, 0, :, :])
            split(wo_h[:, 1, :, :], wo_l[:, 1, :, :], st_o[:, 1, :, :], 0.5)
            chain(dve.tensor_scalar(bias[:, 0:2, :], bias_in[:, 0:2, :], 0.5, None, ALU.mult))
            chain(dve.tensor_copy(bias[:, 2, :], bias_in[:, 2, :]))
            chain(dve.memset(gain[:, 0, :], 2.0))
            for k in range(KC):
                chain(dve.tensor_scalar(state[:, k, :], gain[:, 0, :], c_in[:, k:k + 1], None, ALU.mult))
            chain(dve.tensor_copy(s_h[:, :, :], state[:, :, :]))
            assert count[0] == N_SETUP, count[0]
            for k in range(KC):
                dve.tensor_tensor(s_l[:, k, :], state[:, k, :], s_h[:, k, :].bitcast(F32), ALU.subtract).then_inc(s_lo, 1)

            def step_lo(t, k):
                dve.wait_ge(xs_hi, t * 2 + k + 1)
                dve.tensor_tensor(xt_l[:, k, :], work[k][:, :], xt_h[:, k, :].bitcast(F32), ALU.subtract).then_inc(xs_lo, 1)

            def keep_hpre(t):
                dve.wait_ge(hp_full, t * 2 + 2)
                dve.tensor_copy(hpre[:, t, 2:4, :], work[1][:, :].rearrange("p (c n) -> p c n", c=2)).then_inc(hp_done, 1)

            def keep_state(t, k):
                dve.wait_ge(gate_done, t * 6 + 3 * k + 1)
                dve.scalar_tensor_tensor(keep[:, k, :], act_out[:, k, 0, :], 1.0, state[:, k, :], ALU.add, ALU.mult).then_inc(kept, 1)

            def add_gain(t, k):
                dve.wait_ge(gate_done, t * 6 + 3 * k + 3)
                dve.scalar_tensor_tensor(gain[:, k, :], act_out[:, k, 1, :], 1.0, act_out[:, k, 2, :], ALU.add, ALU.mult).then_inc(gained, 1)
                dve.wait_ge(kept, t * 2 + k + 1)
                dve.wait_ge(gained, t * 2 + k + 1)
                dve.scalar_tensor_tensor(state[:, k, :], keep[:, k, :], 0.5, gain[:, k, :], ALU.mult, ALU.add).then_inc(s_done, 1)

            def state_lo(t, k):
                dve.wait_ge(s_hi, t * 2 + k + 1)
                dve.tensor_tensor(s_l[:, k, :], state[:, k, :], s_h[:, k, :].bitcast(F32), ALU.subtract).then_inc(s_lo, 1)

            step_lo(0, 0)
            step_lo(0, 1)
            keep_hpre(0)

            def step(t, more):
                keep_state(t, 0)
                add_gain(t, 0)
                keep_state(t, 1)
                state_lo(t, 0)
                add_gain(t, 1)
                if more:
                    step_lo(t + 1, 0)
                state_lo(t, 1)
                if more:
                    step_lo(t + 1, 1)
                    keep_hpre(t + 1)

            with dve.Fori(0, T - 1) as t:
                step(t, True)
            step(T - 1, False)
            for i in range(2):
                dve.wait_ge(co_full, i + 1)
                dve.tensor_copy(c_out[:, 2 * i:2 * i + 2, :], work[i][:, :].rearrange("p (c n) -> p c n", c=2)).then_inc(co_done, 1)
            dve.wait_ge(co_done, 2)
            dve.tensor_tensor(c_out[:, :, :], c_out[:, :, :], bo_row[:, :].unsqueeze(1).to_broadcast([P, TC, H]), ALU.add).then_inc(co_done, 1)

            def sum_and_stats(t2, i):
                t = t2 * 2 + i
                dve.wait_ge(tanh_done, t + 1)
                dve.wait_ge(in_back[i], t2 * 16 + 16)
                if not isinstance(t2, int):
                    dve.wait_ge(out_sem[i], t2 * 16)
                dve.tensor_tensor(summed[:, i, :, :], x_back[:, i, :, :], hpre[:, t, :, :], ALU.add).then_inc(sum_done, 1)
                dve.wait_ge(sum_done, t + 1)
                for c in range(TC):
                    dve.bn_stats(stats[:, i, c, :], summed[:, i, c, :]).then_inc(bn_done, 1)
                dve.wait_ge(bn_done, t2 * (2 * TC) + TC * (i + 1))
                dve.memset(fence[:, :], 0.0)
                for c in range(TC):
                    dve.bn_aggr(mv[:, i, c, :], stats[:, i, c, :]).then_inc(mv_done, 1)

            for i in range(2):
                sum_and_stats(0, i)
            with dve.Fori(1, T // 2) as t2:
                for i in range(2):
                    sum_and_stats(t2, i)

        @block.tensor
        def _(pe):
            pe.wait_ge(setup, N_SETUP)
            parts = [(0, 0), (1, 0), (0, 1)]

            def transpose_step(t, first):
                pe.wait_ge(x_in, t * 16 + 16)
                for k in range(KC):
                    if not first:
                        pe.wait_ge(hp_done, t * 2)
                    for c in range(TC):
                        last = pe.transpose(work[k][:, P * c:P * c + P], x_step[:, c, P * k:P * k + P], id_sb[:, :])
                    last.then_inc(xs_full, 1)

            def tokens_by(i, lhs, w, done):
                for j in range(2):
                    c = 2 * i + j
                    terms = [(k, a, d) for k in range(KC) for a, d in parts]
                    for m, (k, a, d) in enumerate(terms):
                        last = pe.matmul(work[i][:, H * j:H * j + H], lhs[a][:, k, P * c:P * c + P], (wo_h, wo_l)[d][:, w, k, :],
                                         start=(m == 0), stop=(m == len(terms) - 1))
                last.then_inc(done, 1)

            def gates_of(n, k, lhs, rhs, start, stop):
                g, mc = n % GATES, n // GATES
                for m, (a, d) in enumerate(parts):
                    last = pe.matmul(gate_ps[n][:, :], lhs[a][:, g, k, P * mc:P * mc + P], rhs[d][:, k, :],
                                     start=start and m == 0, stop=stop and m == len(parts) - 1)
                return last

            def from_x(t, first):
                pe.wait_ge(xs_lo, t * 2 + 2)
                for i in range(2):
                    tokens_by(i, (xt_h, xt_l), 0, hp_full)
                for n in range(GATES * KC):
                    if not first:
                        pe.wait_ge(gate_done, t * 6 - 5 + n)
                    for k in range(KC):
                        gates_of(n, k, (wx_h, wx_l), (xt_h, xt_l), k == 0, False)

            def from_state(t):
                for k in range(KC):
                    pe.wait_ge(s_lo, t * 2 + k + 1)
                    for n in range(GATES * KC):
                        last = gates_of(n, k, (uc_h, uc_l), (s_h, s_l), False, k == KC - 1)
                        if k == KC - 1:
                            last.then_inc(gate_full, 1)

            transpose_step(0, True)
            from_x(0, True)
            with pe.Fori(0, T - 1) as t:
                from_state(t)
                transpose_step(t + 1, False)
                from_x(t + 1, False)
            from_state(T - 1)
            pe.wait_ge(s_lo, 2 * T + 2)
            pe.wait_ge(hp_done, 2 * T)
            for i in range(2):
                tokens_by(i, (s_h, s_l), 1, co_full)


def build(nc, x, Wq, Wkv_short, Wkv_long, Wo, mix, decay, wx, uc, gate_bias, wo, uo, bo, in_c,
          ident, absdiff, qrows, krows, kab, out):
    x1 = nc.dram_tensor("x1_dram", [B, L, H], F32, kind="Internal").ap()
    attention_phase(nc, x, x1, Wq, Wkv_short, Wkv_long, Wo, mix, decay, ident, absdiff, qrows, krows, kab)
    recurrence_phase(nc, x1, wx, uc, gate_bias, wo, uo, bo, in_c, ident, out)


def constants():
    import numpy as np

    pos = np.arange(L, dtype=np.float32)
    chunk = np.arange(L) // P
    rows = ROWS - BIAS_ROW
    q = np.zeros((rows, 2, L), np.float32)
    k = np.zeros((rows, L), np.float32)
    kab = np.zeros((rows, 4), np.float32)
    for c in range(TC):
        sign, own = np.sign(chunk - c).astype(np.float32), (chunk == c).astype(np.float32)
        q[4 * c], q[4 * c + 1], q[4 * c + 2], q[4 * c + 3] = (t for t in (sign * pos, sign * pos, sign, sign))
        q[4 * c:4 * c + 4, 1] = 0
        k[4 * c:4 * c + 2], k[4 * c + 2:4 * c + 4] = -own, own * pos
    kab[:4 * TC, 0] = 1
    kab[4 * TC:, 1] = 1
    kab[1:4 * TC:2, 2] = -1
    q[MAX_ROW - BIAS_ROW, 1] = 1
    k[MAX_ROW - BIAS_ROW + 1] = 1
    q[MAX_ROW - BIAS_ROW:, 0] = 0
    return {"ident": np.eye(P, dtype=np.float32), "absdiff": np.abs(np.arange(P)[:, None] - np.arange(P)).astype(np.float32),
            "qrows": q.reshape(rows, 2 * L), "krows": k, "kab": kab}


def kernel(**inputs):
    import numpy as np
    import concourse.bacc as bacc
    from concourse.bass_utils import run_bass_kernel_spmd

    own = {k.removeprefix("L0_"): np.asarray(v) for k, v in inputs.items()}
    by_partition = lambda a: np.moveaxis(a.reshape(*a.shape[:-1], KC, P), -1, 0)
    t = lambda n: np.ascontiguousarray(own[n].T)
    arrays = {
        "x": own["attn_x"], "Wq": own["attn_Wq"], "Wkv_short": own["attn_Wkv_short"], "Wkv_long": own["attn_Wkv_long"],
        "Wo": own["attn_Wo"], "mix": own["attn_mix_weight"].reshape(1), "decay": own["attn_decay_factor"].reshape(1),
        "wx": np.stack([t("ffn_wf"), t("ffn_wi"), t("ffn_wc")]), "uc": np.stack([t("ffn_uf"), t("ffn_ui"), t("ffn_uc")]),
        "gate_bias": by_partition(np.stack([own["ffn_bf"], own["ffn_bi"], own["ffn_bc"]])),
        "wo": t("ffn_wo"), "uo": t("ffn_uo"), "bo": own["ffn_bo"], "in_c": by_partition(own["ffn_in_c"]),
    } | constants()
    arrays = {f"in_{k}": np.ascontiguousarray(v) for k, v in arrays.items()}
    nc = bacc.Bacc("TRN2", target_bir_lowering=False, num_devices=1)
    args = [nc.dram_tensor(k, v.shape, mybir.dt.from_np(v.dtype), kind="ExternalInput").ap() for k, v in arrays.items()]
    out = nc.dram_tensor("out", (B, L, H), F32, kind="ExternalOutput").ap()
    build(nc, *args, out)
    result = run_bass_kernel_spmd(nc, [arrays], core_ids=[0])
    return result.results[0]["out"]
```

```python
import concourse.bass as bass
from concourse import mybir
from concourse.alu_op_type import AluOpType as ALU
from contextlib import ExitStack

F32 = mybir.dt.float32
F32R = mybir.dt.float32r
ACT = mybir.ActivationFunctionType

B, L, H = 16, 512, 256
P = 128
NH = 16
HD = H // NH
TC = L // P
KC = H // P
GH = 4
GATES = 3
UNITS = 2 * NH // GH
SLOTS = UNITS * TC
RING = 4
AHEAD = 8
SCALE = 0.25
LEAD = 3
BACK = 4
EPS = 1e-5

BIAS_ROW = 3 * HD
ZERO_ROW = BIAS_ROW + 4 * TC
MAX_ROW = ZERO_ROW + 1
ROWS = MAX_ROW + 2
VW = HD + 1
VHALF = 8 * VW + HD - 1

TASKS = {0: ("v", 2, 0), 3: ("v", 3, 0), 4: ("ot", 0, -1), 7: ("ot", 1, -1), 8: ("xt", 0, 1), 11: ("xt", 1, 1),
         12: ("kq", 0, 1), 15: ("kq", 1, 1), 16: ("kq", 2, 1), 19: ("wo", 0, -1), 20: ("wo", 1, -1),
         23: ("v", 0, 1), 24: ("v", 1, 1), 27: ("kq", 3, 1), 28: ("kq", 4, 1), 31: ("kq", 5, 1),
         2: ("pvt", UNITS - 1, -1)}
TASKS |= {4 * u + 6: ("pvt", u, 0) for u in range(UNITS - 1)}
TASKS |= {4 * u - 3: ("shift", u, 0) for u in range(1, UNITS)} | {SLOTS - 3: ("shift", 0, 1)}
COUNT = {"v": 4, "ot": 2, "wo": 2, "xt": 2, "kq": 6, "pvt": UNITS, "shift": UNITS}


def exists(b):
    return not isinstance(b, int) or 0 <= b < B


def wait(eng, sem, b, per, k):
    value = b * per + k
    if isinstance(value, int) and value <= 0:
        return
    eng.wait_ge(sem, value)


def bodies(eng, body):
    body(-1)
    body(0)
    with eng.Fori(1, B - 1) as b:
        body(b)
    body(B - 1)
    body(B)


def unit_of(b, u):
    return (b, u) if u < UNITS else (b + 1, u - UNITS)


def attention_phase(nc, shared, x, x1, Wq, Wks, Wkl, Wo, mix, decay, wx, uc, gate_bias, wo, uo, bo, in_c, ident, absdiff, qrows, krows, kab):
    ctx = ExitStack()
    with ctx:
        sb = lambda n, s, d=F32: ctx.enter_context(nc.sbuf_tensor(n, s, d))
        pb = lambda n, s: ctx.enter_context(nc.psum_tensor(n, s, F32))
        sem = lambda n: ctx.enter_context(nc.semaphore(n))

        w_hi, w_lo = sb("w_hi", [P, 4, KC, H], F32R), sb("w_lo", [P, 4, KC, H], F32R)
        wv_hi, wv_lo = sb("wv_hi", [P, KC, 2, 2, P], F32R), sb("wv_lo", [P, KC, 2, 2, P], F32R)
        x_in, probs, id_sb, x1_stored = shared.x_step, shared.probs, shared.ident, shared.x1_stored
        x_res = sb("x_res", [P, TC, H])
        xt_h, xt_l = sb("xt_h", [P, KC, L], F32R), sb("xt_l", [P, KC, L], F32R)
        kq_h, kq_l = sb("kq_h", [P, 3, 2, L], F32R), sb("kq_l", [P, 3, 2, L], F32R)
        k_op = [sb(f"k_op{i}", [ROWS, GH, L], F32R) for i in range(RING)]
        q_op = [sb(f"q_op{i}", [ROWS, GH, L], F32R) for i in range(RING)]
        vals = sb("vals", [P, TC, 2, 2, VHALF])
        maxes = sb("maxes", [P, 2, TC, GH])
        shift_row = sb("shift_row", [GH, 2, L], F32R)
        pv_sb = sb("pv_sb", [P, 2, L])
        rden, rdena = sb("rden", [P, 2, TC, GH]), sb("rdena", [P, 2, TC, GH])
        o_att = [sb(f"o_att{a}", [P, TC, NH, HD]) for a in range(2)]
        o_sum = sb("o_sum", [P, TC, H])
        ot_h, ot_l = sb("ot_h", [P, KC, L], F32R), sb("ot_l", [P, KC, L], F32R)
        res = sb("res", [P, TC, H])
        stats, mv = sb("stats", [P, TC, 6]), sb("mv", [P, TC, 2])
        veps, rstd, nmr = (sb(n, [P, TC]) for n in ("veps", "rstd", "nmr"))
        consts = sb("consts", [P, 3, TC])
        id_r = sb("id_r", [P, P], F32R)
        dist = sb("dist", [P, P])
        dist_h, dist_l = sb("dist_h", [P, P], F32R), sb("dist_l", [P, P], F32R)
        small = sb("small", [P, 8])
        kab_sb = sb("kab_sb", [ROWS - BIAS_ROW, 4])
        NR = ROWS - BIAS_ROW

        stage = probs[:, :, :, :].rearrange("p a h n -> p (a h n)")
        st_q = stage[:, 0:512].rearrange("p (k n) -> p k n", k=KC)
        st_kv = [stage[:, 512 + 1024 * a:1536 + 1024 * a].rearrange("p (k n) -> p k n", k=KC) for a in range(2)]
        st_o = stage[:, 2560:3072].rearrange("p (k n) -> p k n", k=KC)
        rows_in = o_sum[:, :, :].rearrange("p t n -> p (t n)")
        rows_tmp = res[:, :, :].rearrange("p t n -> p (t n)")
        rows_out = ot_h[:, :, :].rearrange("p k n -> p (k n)")
        rows_h = ot_l[:, :, :].rearrange("p k n -> p (k n)")

        b_ps = [pb(f"b_ps{i}", [P, 2, L]) for i in range(2)]
        a_ps = [pb(f"a_ps{i}", [P, L]) for i in range(2)]
        pv_ps = pb("pv_ps", [P, L])
        work = pb("work", [P, L])

        const_in, rows_set, setup, ones_set, exp_mix = map(sem, ("const_in", "rows_set", "setup", "ones_set", "exp_mix"))
        x_loaded, res_loaded = map(sem, ("x_loaded", "res_loaded"))
        k_loaded = [sem(f"k_loaded{i}") for i in range(RING)]
        q_loaded = [sem(f"q_loaded{i}") for i in range(RING)]
        shift_loaded = [sem(f"shift_loaded{i}") for i in range(2)]
        full = {n: sem(f"{n}_full") for n in COUNT}
        b_full, a_full, pv_full = map(sem, ("b_full", "a_full", "pv_full"))
        a_reduced, exp_done, pv_copied = map(sem, ("a_reduced", "exp_done", "pv_copied"))
        xt_hi, kq_hi, ot_hi = map(sem, ("xt_hi", "kq_hi", "ot_hi"))
        rden_done, rdena_done, osum_done, bn_done, mv_done = map(sem, ("rden_done", "rdena_done", "osum_done", "bn_done", "mv_done"))
        ln_step, normed = map(sem, ("ln_step", "normed"))
        done = {n: sem(f"{n}_done") for n in COUNT}
        N_SETUP = 30

        block = ctx.enter_context(nc.Block())

        @block.sync
        def _(sp):
            copy_words = lambda dst, src: sp.dma_start(dst.bitcast(F32), src.bitcast(F32))
            for dst, src in ((st_q, Wq.rearrange("(k p) n -> p k n", p=P)), (st_kv[0], Wkl.rearrange("(k p) n -> p k n", p=P)),
                             (st_kv[1], Wks.rearrange("(k p) n -> p k n", p=P)), (st_o, Wo.rearrange("(k p) n -> p k n", p=P)),
                             (id_sb[:, :], ident), (dist[:, :], absdiff),
                             (rows_in[0:NR, 0:L], krows), (rows_tmp[0:NR, 0:2 * L], qrows), (kab_sb[:, :], kab),
                             (small[:, 0:1], mix.unsqueeze(0).to_broadcast([P, 1])), (small[:, 1:2], decay.unsqueeze(0).to_broadcast([P, 1]))):
                sp.dma_start(dst, src).then_inc(const_in, 16)
            sp.wait_ge(setup, N_SETUP)
            for h in range(GH):
                for i in range(RING):
                    copy_words(q_op[i][BIAS_ROW:MAX_ROW, h, :], rows_h[0:NR - 2, 0:L]).then_inc(rows_set, 16)
                for i in range(RING):
                    copy_words(k_op[i][BIAS_ROW:ROWS, h, :], rows_out[0:NR, (1 - i % 2) * L:(2 - i % 2) * L]).then_inc(rows_set, 16)

            def load_rows(dst, h, part, half, pos, order, s):
                at = pos + HD * h
                for r, src in enumerate(order):
                    copy_words(dst[HD * r:HD * r + HD, h, :], src[at:at + HD, part, half, :]).then_inc(s, 16)

            def projected(b, n):
                if isinstance(b, int):
                    wait(sp, done["kq"], b, 6, n)

            def load_k(b, u, h):
                if exists(b):
                    g, att = u // 2, u % 2
                    if h == 0:
                        projected(b, 3 * (g // 2) + 2 * att + 1)
                        wait(sp, b_full, b, 2 * SLOTS, 8 * (u - RING + 1))
                    load_rows(k_op[u % RING], h, 2 * att, g // 2, 64 * (g % 2), (kq_h, kq_l, kq_h), k_loaded[u % RING])

            def load_q(b, g, h):
                if exists(b):
                    if h == 0:
                        projected(b, 3 * (g // 2) + 2)
                        wait(sp, b_full, b, 2 * SLOTS, 2 * (8 * g - 14))
                    load_rows(q_op[g], h, 1, g // 2, 64 * (g % 2), (kq_h, kq_h, kq_l), q_loaded[g])

            def body(b):
                for s in range(SLOTS):
                    if s % 4 == 0:
                        for h in range(GH):
                            load_k(*unit_of(b, s // 4 + 3), h)
                    if s % 8 == 2:
                        bb, u = unit_of(b, (s + 14) // 4)
                        for h in range(GH):
                            load_q(bb, u // 2, h)
                    if s in TASKS and TASKS[s][0] == "shift":
                        _, u, off = TASKS[s]
                        bb = b + off
                        if exists(bb):
                            wait(sp, done["shift"], bb, UNITS, u + 1)
                            for h in range(GH):
                                copy_words(q_op[u // 2][MAX_ROW + u % 2:MAX_ROW + u % 2 + 1, h, :],
                                           shift_row[h:h + 1, u % 2, :]).then_inc(shift_loaded[u % 2], 16)

            bodies(sp, body)
            sp.wait_ge(full["xt"], 2 * B)
            sp.wait_ge(x1_stored, 16 + 16 * (B - 1))
            sp.dma_start(x_in[:, :, :], x1[0].rearrange("(c p) n -> p c n", p=P)).then_inc(shared.x_in, 16)
            sp.wait_ge(pv_full, B * SLOTS)
            for g, w in enumerate((wo, uo)):
                sp.dma_start(shared.stage_o[:, g, :, :], w.rearrange("(k p) n -> p k n", p=P)).then_inc(shared.output_in, 16)
            for g in range(GATES):
                sp.dma_start(shared.stage_w[:, g, :, :], wx[g].rearrange("(k p) n -> p k n", p=P)).then_inc(shared.wx_in, 16)
            for g in range(GATES):
                sp.dma_start(shared.stage_u[:, g, :, :], uc[g].rearrange("(k p) n -> p k n", p=P)).then_inc(shared.uc_in, 16)
            sp.dma_start(shared.bias_in[:, :, :], gate_bias).then_inc(shared.params_in, 16)
            sp.dma_start(shared.c_in[:, :], in_c).then_inc(shared.params_in, 16)
            sp.dma_start(shared.bo_row[:, :], bo.unsqueeze(0).to_broadcast([P, H])).then_inc(shared.params_in, 16)

        @block.gpsimd
        def _(pool):
            for n, value in ((0, EPS), (1, -0.5), (2, -1.0)):
                pool.memset(consts[:, n, :], value).then_inc(ln_step, 1)
            pool.wait_ge(ln_step, 3)
            pool.memset(nmr[:, :], 0.0).then_inc(x1_stored, 16)

            def body(b):
                bb = b - 1
                if exists(bb):
                    wait(pool, done["pvt"], bb, UNITS, UNITS)
                    pool.tensor_tensor(o_sum[:, :, :], o_att[0][:, :, :, :].rearrange("p t h d -> p t (h d)"),
                                       o_att[1][:, :, :, :].rearrange("p t h d -> p t (h d)"), ALU.add).then_inc(osum_done, 1)
                    wait(pool, mv_done, bb, TC, TC)
                    pool.tensor_tensor(veps[:, :], mv[:, :, 1], consts[:, 0, :], ALU.add).then_inc(ln_step, 1)
                    wait(pool, ln_step, bb, 4, 3 + 1)
                    pool.tensor_tensor(rstd[:, :], veps[:, :], consts[:, 1, :], ALU.pow).then_inc(ln_step, 1)
                    pool.tensor_tensor(nmr[:, :], mv[:, :, 0], consts[:, 2, :], ALU.mult).then_inc(ln_step, 1)
                    wait(pool, ln_step, bb, 4, 3 + 3)
                    pool.tensor_tensor(nmr[:, :], nmr[:, :], rstd[:, :], ALU.mult).then_inc(ln_step, 1)

            bodies(pool, body)

        @block.scalar
        def _(act):
            act.wait_ge(const_in, 11 * 16)
            act.activation(small[:, 2:3], small[:, 0:1], ACT.Exp, scale=-1.0).then_inc(exp_mix, 1)

            def exp_pair(b, s, hp):
                wait(act, b_full, b, 2 * SLOTS, 2 * s + hp + 1)
                wait(act, pv_full, b, SLOTS, s - 1)
                act.activation(probs[:, s % 2, 2 * hp:2 * hp + 2, :], b_ps[hp][:, :, :], ACT.Exp).then_inc(exp_done, 1)

            def body(b):
                for s in range(SLOTS):
                    if s == 1 and exists(b + 1):
                        act.dma_start(x_in[:, :, :], x[b + 1].rearrange("(t p) n -> p t n", p=P)).then_inc(x_loaded, 16)
                    if s == 21 and exists(b):
                        wait(act, done["wo"], b, 2, 0)
                        act.dma_start(x_res[:, :, :], x[b].rearrange("(t p) n -> p t n", p=P)).then_inc(res_loaded, 16)
                    if s == 25 and exists(b - 1):
                        wait(act, ln_step, b - 1, 4, 3 + 4)
                        for t in range(TC):
                            act.activation(res[:, t, :], res[:, t, :], ACT.Identity, bias=nmr[:, t:t + 1],
                                           scale=rstd[:, t:t + 1]).then_inc(normed, 1)
                        wait(act, normed, b - 1, TC, TC)
                        act.dma_start(x1[b - 1].rearrange("(t p) n -> p t n", p=P), res[:, :, :]).then_inc(x1_stored, 16)
                    if exists(b):
                        exp_pair(b, s, 0)
                        exp_pair(b, s, 1)
                    if s not in TASKS or not exists(b + TASKS[s][2]):
                        continue
                    kind, n, off = TASKS[s]
                    bb = b + off
                    if kind in ("xt", "kq", "ot"):
                        dst, ready, scale = {"xt": (xt_h[:, n % 2, :], xt_hi, 1.0), "ot": (ot_h[:, n % 2, :], ot_hi, 1.0),
                                             "kq": (kq_h[:, n % 3, n // 3, :], kq_hi, SCALE if n % 3 == 1 else 1.0)}[kind]
                        wait(act, full[kind], bb, COUNT[kind], n + 1)
                        act.activation(dst, work[:, :], ACT.Copy, scale=scale).then_inc(ready, 1)
                    if kind == "v":
                        wait(act, full["v"], bb, 4, n + 1)
                        if n == 2:
                            wait(act, pv_full, bb, SLOTS, 0)
                        for j in range(2):
                            src = work[:, 256 * j:256 * j + 256].rearrange("p (a h d) -> p a h d", a=2, d=HD)
                            dst = vals[:, 2 * (n % 2) + j, n // 2, :, 0:8 * VW].rearrange("p a (h e) -> p a h e", e=VW)[:, :, :, 0:HD]
                            act.activation(dst, src, ACT.Copy).then_inc(done["v"], 1)

            bodies(act, body)
            act.wait_ge(x1_stored, 16 * B)

        @block.vector
        def _(dve):
            step = [0]

            def chain(instruction):
                step[0] += 1
                instruction.then_inc(setup, 1)
                dve.wait_ge(setup, step[0])

            def split(hi, lo, value, factor=1.0):
                chain(dve.tensor_scalar(hi, value, factor, None, ALU.mult))
                chain(dve.scalar_tensor_tensor(lo, value, factor, hi.bitcast(F32), ALU.mult, ALU.subtract))

            dve.memset(vals[:, :, :, :, :], 1.0).then_inc(ones_set, 1)
            dve.wait_ge(const_in, 11 * 16)
            split(w_hi[:, 0, :, :], w_lo[:, 0, :, :], st_q)
            for a in range(2):
                split(w_hi[:, 1 + a, :, :], w_lo[:, 1 + a, :, :], st_kv[a][:, :, 0:H])
                for k in range(KC):
                    split(wv_hi[:, k, :, a, :], wv_lo[:, k, :, a, :], st_kv[a][:, k, H:2 * H].rearrange("p (f n) -> p f n", f=2))
            split(w_hi[:, 3, :, :], w_lo[:, 3, :, :], st_o)
            dve.wait_ge(exp_mix, 1)
            chain(dve.tensor_scalar(small[:, 3:4], small[:, 2:3], 1.0, None, ALU.add))
            chain(dve.reciprocal(small[:, 5:6], small[:, 3:4]))
            chain(dve.tensor_scalar(small[:, 4:5], small[:, 5:6], -1.0, 1.0, ALU.mult, ALU.add))
            chain(dve.tensor_scalar(small[:, 6:7], small[:, 1:2], -1.0, 1.0, ALU.mult, ALU.add))
            chain(dve.tensor_scalar(dist[:, :], dist[:, :], small[:, 6:7], -1.0, ALU.mult, ALU.mult))
            split(dist_h[:, :], dist_l[:, :], dist[:, :])
            chain(dve.tensor_scalar(kab_sb[:, 3:4], kab_sb[:, 0:1], small[0:NR, 6:7], kab_sb[:, 1:2], ALU.mult, ALU.add))
            chain(dve.tensor_scalar(rows_in[0:NR, L:2 * L], rows_in[0:NR, 0:L], kab_sb[:, 3:4], None, ALU.mult))
            chain(dve.tensor_copy(id_r[:, :], id_sb[:, :]))
            chain(dve.tensor_copy(rows_h[0:NR, L:2 * L], rows_in[0:NR, L:2 * L]))
            chain(dve.scalar_tensor_tensor(rows_out[0:NR, 0:L], rows_h[0:NR, L:2 * L].bitcast(F32), kab_sb[:, 2:3],
                                           rows_in[0:NR, L:2 * L], ALU.mult, ALU.add))
            chain(dve.tensor_copy(rows_out[0:NR, L:2 * L], rows_tmp[0:NR, L:2 * L]))
            chain(dve.tensor_copy(rows_h[0:NR, 0:L], rows_tmp[0:NR, 0:L]))
            assert step[0] == N_SETUP, step[0]

            def rest(dst, hi, sem_hi, kind, bb, n, scale):
                wait(dve, sem_hi, bb, COUNT[kind], n + 1)
                dve.scalar_tensor_tensor(dst, work[:, :], scale, hi.bitcast(F32), ALU.mult, ALU.subtract).then_inc(done[kind], 1)

            def body(b):
                for s in range(SLOTS):
                    if s == 22 and exists(b - 1):
                        wait(dve, bn_done, b - 1, TC, TC)
                    bb, u = unit_of(b, (s + AHEAD) // 4)
                    def reduce(h, bb=bb, u=u, s=s):
                        if exists(bb):
                            wait(dve, a_full, bb, 16 * UNITS, 16 * u + 4 * (s % 4) + h + 1)
                            dve.reduce_max(maxes[:, u % 2, s % 4, h:h + 1], a_ps[h % 2][:, :],
                                           mybir.AxisListType.X).then_inc(a_reduced, 1)

                    by_scalar = s in TASKS and TASKS[s][0] in ("xt", "kq", "ot")
                    for h in range(3 if by_scalar else 2):
                        reduce(h)
                    if s in TASKS and exists(b + TASKS[s][2]):
                        kind, n, off = TASKS[s]
                        bb = b + off
                        if kind == "xt":
                            rest(xt_l[:, n, :], xt_h[:, n, :], xt_hi, kind, bb, n, 1.0)
                        if kind == "kq":
                            rest(kq_l[:, n % 3, n // 3, :], kq_h[:, n % 3, n // 3, :], kq_hi, kind, bb, n, SCALE if n % 3 == 1 else 1.0)
                        if kind == "ot":
                            rest(ot_l[:, n, :], ot_h[:, n, :], ot_hi, kind, bb, n, 1.0)
                        if kind == "shift":
                            wait(dve, full["shift"], bb, UNITS, n + 1)
                            wait(dve, shift_loaded[n % 2], bb, 64 * UNITS // 2, 64 * (n // 2))
                            dve.tensor_scalar(shift_row[:, n % 2, :], work[0:GH, :], -1.0, None, ALU.mult).then_inc(done["shift"], 1)
                        if kind == "pvt":
                            g, att = n // 2, n % 2
                            o = work[:, :].rearrange("p (t h e) -> p t h e", t=TC, h=GH)
                            wait(dve, full["pvt"], bb, UNITS, n + 1)
                            dve.reciprocal(rden[:, att, :, :], o[:, :, :, HD]).then_inc(rden_done, 1)
                            wait(dve, rden_done, bb, UNITS, n + 1)
                            dve.tensor_scalar(rdena[:, att, :, :], rden[:, att, :, :], small[:, 4 + att:5 + att], None,
                                              ALU.mult).then_inc(rdena_done, 1)
                            wait(dve, rdena_done, bb, UNITS, n + 1)
                            if n < 2:
                                wait(dve, osum_done, bb, 1, 0)
                            dve.tensor_tensor(o_att[att][:, :, GH * g:GH * g + GH, :], o[:, :, :, 0:HD],
                                              rdena[:, att, :, :].unsqueeze(3).to_broadcast([P, TC, GH, HD]),
                                              ALU.mult).then_inc(done["pvt"], 1)
                        if kind == "wo":
                            wait(dve, full["wo"], bb, 2, n + 1)
                            wait(dve, res_loaded, bb, 16, 16)
                            wait(dve, x1_stored, bb, 16, 16)
                            r = res[:, 2 * n:2 * n + 2, :]
                            dve.tensor_tensor(r, work[:, :].rearrange("p (t n) -> p t n", t=2), x_res[:, 2 * n:2 * n + 2, :],
                                              ALU.add).then_inc(done["wo"], 1)
                            wait(dve, done["wo"], bb, 2, n + 1)
                            for j in range(2):
                                dve.bn_stats(stats[:, 2 * n + j, :], res[:, 2 * n + j, :]).then_inc(bn_done, 1)
                    for h in range(3 if by_scalar else 2, GH):
                        reduce(h)
                    if s == 22 and exists(b - 1):
                        for t in range(TC):
                            dve.bn_aggr(mv[:, t, :], stats[:, t, :]).then_inc(mv_done, 1)
                    if s % 4 == 0:
                        bb, u = (b, s // 4 - 1) if s else (b - 1, UNITS - 1)
                        if exists(bb):
                            wait(dve, pv_full, bb, SLOTS, 4 * u + 4)
                            dve.tensor_copy(pv_sb[:, u % 2, :], pv_ps[:, :]).then_inc(pv_copied, 1)

            bodies(dve, body)

        @block.tensor
        def _(pe):
            pe.wait_ge(ones_set, 1)
            pe.wait_ge(setup, N_SETUP)
            pe.wait_ge(rows_set, 16 * GH * 2 * RING)

            def three(out, lhs, rhs):
                last = None
                pairs = [(k, a, c) for k in range(KC) for a, c in ((0, 0), (1, 0), (0, 1))]
                for i, (k, a, c) in enumerate(pairs):
                    last = pe.matmul(out, lhs(a, k), rhs(c, k), start=(i == 0), stop=(i == len(pairs) - 1))
                return last

            def score(out, lhs, rhs, chunk, rows, diagonals):
                last = pe.matmul(out, lhs[0:rows, P * chunk:P * chunk + P], rhs[0:rows, :], start=True, stop=not diagonals)
                for i, d in enumerate(diagonals):
                    last = pe.matmul(out[:, P * chunk:P * chunk + P], id_r[:, :], d[:, :], start=False, stop=(i == len(diagonals) - 1))
                return last

            def score_pair(b, s, hp):
                u, c = s // 4, s % 4
                q, k = q_op[u // 2], k_op[u % RING]
                if c == 0 and hp == 0:
                    wait(pe, shift_loaded[u % 2], b, 64 * UNITS // 2, 64 * (u // 2 + 1))
                wait(pe, exp_done, b, 2 * SLOTS, 2 * s + hp - 1)
                for j in range(2):
                    h = 2 * hp + j
                    last = score(b_ps[hp][:, j, :], k[:, h, :], q[:, h, :], c, ROWS - 1 + u % 2, (dist_h, dist_l) if u % 2 else ())
                last.then_inc(b_full, 1)

            def score_for_max(b, s, h):
                bb, u = unit_of(b, (s + AHEAD) // 4)
                c = s % 4
                if not exists(bb):
                    return
                q, k = q_op[u // 2], k_op[u % RING]
                if c == 0 and h == 0:
                    wait(pe, k_loaded[u % RING], bb, 384, 192 * (u // RING + 1))
                    wait(pe, q_loaded[u // 2], bb, 192, 192)
                wait(pe, a_reduced, bb, 16 * UNITS, 16 * u + 4 * c + h - 1)
                score(a_ps[h % 2][:, :], q[:, h, :], k[:, h, :], c, MAX_ROW, (dist_h,) if u % 2 else ()).then_inc(a_full, 1)

            def weigh(b, s):
                u, c = s // 4, s % 4
                g, att = u // 2, u % 2
                wait(pe, exp_done, b, 2 * SLOTS, 2 * s + 2)
                if c == 0:
                    wait(pe, pv_copied, b, UNITS, u)
                    if u in (0, UNITS // 2):
                        wait(pe, done["v"], b, 8, 4 if u == 0 else 8)
                for h in range(GH):
                    at = VW * (GH * (g % 2) + h)
                    last = pe.matmul(pv_ps[32 * h:32 * h + 32, :], vals[:, c, g // 2, att, at:at + 32], probs[:, s % 2, h, :],
                                     start=(c == 0), stop=(c == TC - 1))
                last.then_inc(pv_full, 1)

            def work_task(b, s):
                kind, n, off = TASKS[s]
                bb = b + off
                if not exists(bb):
                    return
                for back in range(1, SLOTS + 1):
                    at, ob = (s - back, b) if s >= back else (s - back + SLOTS, b - 1)
                    if isinstance(ob, int) and ob < -1:
                        break
                    if at in TASKS and exists(ob + TASKS[at][2]):
                        k0, n0, off0 = TASKS[at]
                        per, m = (8, 2 * n0 + 2) if k0 == "v" else (COUNT[k0], n0 + 1)
                        wait(pe, done[k0], ob + off0, per, m)
                        break
                if kind == "xt":
                    wait(pe, x_loaded, bb, 16, 16)
                    for t in range(TC):
                        last = pe.transpose(work[:, P * t:P * t + P], x_in[:, t, P * n:P * n + P], id_sb[:, :])
                if kind == "kq":
                    w, half = (1, 0, 2)[n % 3], n // 3
                    wait(pe, done["xt"], bb, 2, 2)
                    last = three(work[:, :], lambda a, k: (w_hi, w_lo)[a][:, w, k, P * half:P * half + P],
                                 lambda a, k: (xt_h, xt_l)[a][:, k, :])
                if kind == "v":
                    wait(pe, done["xt"], bb, 2, 2)
                    for j in range(2):
                        t = 2 * (n % 2) + j
                        last = three(work[:, 256 * j:256 * j + 256], lambda a, k: (xt_h, xt_l)[a][:, k, P * t:P * t + P],
                                     lambda a, k: (wv_hi, wv_lo)[a][:, k, n // 2, :, :])
                if kind == "ot":
                    wait(pe, osum_done, bb, 1, 1)
                    for t in range(TC):
                        last = pe.transpose(work[:, P * t:P * t + P], o_sum[:, t, P * n:P * n + P], id_sb[:, :])
                if kind == "wo":
                    wait(pe, done["ot"], bb, 2, 2)
                    for j in range(2):
                        t = 2 * n + j
                        last = three(work[:, 256 * j:256 * j + 256], lambda a, k: (ot_h, ot_l)[a][:, k, P * t:P * t + P],
                                     lambda a, k: (w_hi, w_lo)[a][:, 3, k, :])
                if kind == "pvt":
                    wait(pe, pv_copied, bb, UNITS, n + 1)
                    for t in range(TC):
                        last = pe.transpose(work[:, P * t:P * t + P], pv_sb[:, n % 2, P * t:P * t + P], id_sb[:, :])
                if kind == "shift":
                    wait(pe, a_reduced, bb, 16 * UNITS, 16 * n + 16)
                    for t in range(TC):
                        last = pe.transpose(work[0:GH, P * t:P * t + P], maxes[:, n % 2, t, :], id_sb[:, :])
                last.then_inc(full[kind], 1)

            def body(b):
                for s in range(SLOTS):
                    if exists(b):
                        score_pair(b, s, 0)
                    score_for_max(b, s, 0)
                    if exists(b):
                        score_pair(b, s, 1)
                    score_for_max(b, s, 1)
                    if s in TASKS:
                        work_task(b, s)
                    score_for_max(b, s, 2)
                    bb, ss = (b, s - 1) if s else (b - 1, SLOTS - 1)
                    if exists(bb):
                        weigh(bb, ss)
                    score_for_max(b, s, 3)

            bodies(pe, body)


class Shared:

    def __init__(self, nc, ctx):
        sb = lambda n, s: ctx.enter_context(nc.sbuf_tensor(n, s, F32))
        sem = lambda n: ctx.enter_context(nc.semaphore(n))
        self.ident = sb("ident_sb", [P, P])
        self.x_step = sb("x_step", [P, TC, H])
        self.bias_in, self.c_in, self.bo_row = sb("bias_in", [P, GATES, KC]), sb("c_in", [P, KC]), sb("bo_row", [P, H])
        self.probs = sb("probs", [P, 2, GH, L])
        stage = self.probs[:, :, :, :].rearrange("p a h n -> p (a h n)")
        self.stage_w = stage[:, 0:1536].rearrange("p (g k n) -> p g k n", g=GATES, k=KC)
        self.stage_u = stage[:, 1536:3072].rearrange("p (g k n) -> p g k n", g=GATES, k=KC)
        self.stage_o = stage[:, 3072:4096].rearrange("p (g k n) -> p g k n", g=2, k=KC)
        self.x1_stored, self.x_in, self.output_in, self.wx_in, self.uc_in, self.params_in = map(
            sem, ("x1_stored", "x_step_in", "output_in", "wx_in", "uc_in", "params_in"))


def recurrence_phase(nc, shared, x1, out):
    T = B
    ctx = ExitStack()
    with ctx:
        sb = lambda n, s, d=F32: ctx.enter_context(nc.sbuf_tensor(n, s, d))
        pb = lambda n, s: ctx.enter_context(nc.psum_tensor(n, s, F32))
        sem = lambda n: ctx.enter_context(nc.semaphore(n))

        wx_h, wx_l = sb("wx_h", [P, GATES, KC, H], F32R), sb("wx_l", [P, GATES, KC, H], F32R)
        uc_h, uc_l = sb("uc_h", [P, GATES, KC, H], F32R), sb("uc_l", [P, GATES, KC, H], F32R)
        wo_h, wo_l = sb("wo_h", [P, 2, KC, H], F32R), sb("wo_l", [P, 2, KC, H], F32R)
        hpre = sb("hpre", [P, T, TC, H])
        x_step, id_sb, x_in, bias_in = shared.x_step, shared.ident, shared.x_in, shared.bias_in
        xt_h, xt_l = sb("xs_h", [P, KC, L], F32R), sb("xs_l", [P, KC, L], F32R)
        act_out = sb("act_out", [P, KC, GATES, L])
        state, keep, gain = sb("state", [P, KC, L]), sb("keep", [P, KC, L]), sb("gain", [P, KC, L])
        s_h, s_l = sb("s_h", [P, KC, L], F32R), sb("s_l", [P, KC, L], F32R)
        bias, c_out = sb("bias", [P, GATES, KC]), sb("c_out", [P, TC, H])
        x_back, summed = sb("x_back", [P, BACK, TC, H]), sb("summed", [P, BACK, TC, H])
        stats, mv = sb("stats2", [P, BACK, TC, 6]), sb("mv2", [P, BACK, TC, 2])
        veps, rstd, nmr = (sb(n, [P, BACK, TC]) for n in ("veps2", "rstd2", "nmr2"))
        consts, fence = sb("consts2", [P, 3, TC]), sb("fence", [P, 1])

        gate_ps = [pb(f"gate_ps{i}", [P, L]) for i in range(GATES * KC)]
        work = [pb(f"work2_{i}", [P, L]) for i in range(2)]

        w_hi, w_lo, biased, state_set, state_hi_set, xs_full, xs_hi, xs_lo = map(sem, (
            "w2_hi_done", "w2_lo_done", "biased", "state_set", "state_hi_set", "xs_full", "xs_hi", "xs_lo"))
        hp_full, hp_done, gate_full, gate_done, kept, gained, s_done, s_hi, s_lo = map(sem, (
            "hp_full", "hp_done", "gate_full", "gate_done", "kept", "gained", "s_done", "s_hi_done", "s_lo_done"))
        co_full, co_done, pool_added, dve_added, tanh_done, sum_done, bn_done, mv_done, ln_step, normed = map(sem, (
            "co_full", "co_done", "pool_added", "dve_added", "tanh_done", "sum_done", "bn2_done", "mv2_done", "ln2_step", "normed2"))
        in_back = [sem(f"in_back{i}") for i in range(BACK)]
        stored = [sem(f"stored{i}") for i in range(BACK)]
        pieces = ((shared.output_in, 2, wo_h[:, 0, :, :], wo_l[:, 0, :, :], shared.stage_o[:, 0, :, :], 1.0),
                  (shared.wx_in, GATES, wx_h[:, :, :, :], wx_l[:, :, :, :], shared.stage_w, 1.0),
                  (shared.uc_in, GATES, uc_h[:, :, :, :], uc_l[:, :, :, :], shared.stage_u, 0.5),
                  (shared.output_in, 2, wo_h[:, 1, :, :], wo_l[:, 1, :, :], shared.stage_o[:, 1, :, :], 0.5))

        block = ctx.enter_context(nc.Block())
        tokens = lambda ap: ap.rearrange("(c p) n -> p c n", p=P)

        def rounds(eng, round_of_steps):
            round_of_steps(0, True, False)
            with eng.Fori(1, T // BACK - 1) as r:
                round_of_steps(r, False, False)
            round_of_steps(T // BACK - 1, False, True)

        @block.sync
        def _(sp):
            sp.wait_ge(shared.x1_stored, 16 + 16 * B)
            for t in range(BACK):
                sp.dma_start(x_back[:, t, :, :], tokens(x1[t])).then_inc(in_back[t], 16)
            for t in range(T):
                if t + BACK < T:
                    sp.wait_ge(sum_done, t + 1)
                    sp.dma_start(x_back[:, t % BACK, :, :], tokens(x1[t + BACK])).then_inc(in_back[t % BACK], 16)
                sp.wait_ge(normed, TC * (t + 1))
                sp.dma_start(tokens(out[t]), summed[:, t % BACK, :, :]).then_inc(stored[t % BACK], 16)
            for i in range(BACK):
                sp.wait_ge(stored[i], 16 * T // BACK)

        @block.gpsimd
        def _(pool):
            for n, value in ((0, EPS), (1, -0.5), (2, -1.0)):
                pool.memset(consts[:, n, :], value).then_inc(ln_step, 1)
            pool.wait_ge(ln_step, 3)
            pool.wait_ge(co_done, 3)
            pool.wait_ge(hp_done, 2 * T)

            def add_state(t):
                pool.tensor_tensor(hpre[:, t, 1:TC, :], hpre[:, t, 1:TC, :], c_out[:, 1:TC, :], ALU.add).then_inc(pool_added, 1)

            def scales(r, i, first):
                t = r * BACK + i
                if not first:
                    pool.wait_ge(normed, t * TC - (BACK - 1) * TC)
                pool.wait_ge(mv_done, t * TC + TC)
                pool.tensor_tensor(veps[:, i, :], mv[:, i, :, 1], consts[:, 0, :], ALU.add).then_inc(ln_step, 1)
                pool.wait_ge(ln_step, t * 4 + 3 + 1)
                pool.tensor_tensor(rstd[:, i, :], veps[:, i, :], consts[:, 1, :], ALU.pow).then_inc(ln_step, 1)
                pool.tensor_tensor(nmr[:, i, :], mv[:, i, :, 0], consts[:, 2, :], ALU.mult).then_inc(ln_step, 1)
                pool.wait_ge(ln_step, t * 4 + 3 + 3)
                pool.tensor_tensor(nmr[:, i, :], nmr[:, i, :], rstd[:, i, :], ALU.mult).then_inc(ln_step, 1)

            def round_of_steps(r, first, last):
                for i in range(BACK):
                    if i + LEAD < BACK or not last:
                        add_state(r * BACK + i + LEAD)
                    scales(r, i, first)

            for t in range(LEAD):
                add_state(t)
            rounds(pool, round_of_steps)

        @block.scalar
        def _(act):
            def weight_hi(n):
                loaded, loads, hi, _, value, factor = pieces[n]
                act.wait_ge(loaded, 16 * loads)
                act.activation(hi, value, ACT.Copy, scale=factor).then_inc(w_hi, 1)

            def gate(t, n):
                k, g = n // GATES, n % GATES
                act.wait_ge(gate_full, t * 6 + n + 1)
                act.activation(act_out[:, k, g, :], gate_ps[n][:, :], ACT.Tanh, bias=bias[:, g, k:k + 1],
                               scale=0.5 if g < 2 else 1.0).then_inc(gate_done, 1)

            def state_hi(t, k):
                act.wait_ge(s_done, t * 2 + k + 1)
                act.activation(s_h[:, k, :], state[:, k, :], ACT.Copy).then_inc(s_hi, 1)

            def step_hi(t, k):
                act.wait_ge(xs_full, t * 2 + k + 1)
                act.activation(xt_h[:, k, :], work[k][:, :], ACT.Copy).then_inc(xs_hi, 1)

            def keep_hpre(t):
                act.wait_ge(hp_full, t * 2 + 1)
                act.activation(hpre[:, t, 0:2, :], work[0][:, :].rearrange("p (c n) -> p c n", c=2), ACT.Copy).then_inc(hp_done, 1)

            def load_step(t):
                act.dma_start(x_step[:, :, :], tokens(x1[t])).then_inc(x_in, 16)

            act.wait_ge(shared.x1_stored, 16 + 16 * B)
            step_hi(0, 0)
            step_hi(0, 1)
            load_step(1)
            weight_hi(0)
            weight_hi(1)
            keep_hpre(0)
            weight_hi(2)
            weight_hi(3)
            step_hi(1, 0)
            step_hi(1, 1)
            load_step(2)
            act.wait_ge(biased, 2)

            def step(t, more, further, load):
                for n in range(5):
                    gate(t, n)
                state_hi(t, 0)
                gate(t, 5)
                state_hi(t, 1)
                if more:
                    keep_hpre(t + 1)
                if further:
                    step_hi(t + 2, 0)
                    step_hi(t + 2, 1)
                if load:
                    load_step(t + 3)

            with act.Fori(0, T - 3) as t:
                step(t, True, True, True)
            step(T - 3, True, True, False)
            step(T - 2, True, False, False)
            step(T - 1, False, False, False)

            def tanh_out(t):
                act.wait_ge(pool_added, t + 1)
                act.wait_ge(dve_added, t + 1)
                act.activation(hpre[:, t, :, :], hpre[:, t, :, :], ACT.Tanh).then_inc(tanh_done, 1)

            def normalise(r, i):
                t = r * BACK + i
                act.wait_ge(ln_step, t * 4 + 3 + 4)
                for c in range(TC):
                    act.activation(summed[:, i, c, :], summed[:, i, c, :], ACT.Identity, bias=nmr[:, i, c:c + 1],
                                   scale=rstd[:, i, c:c + 1]).then_inc(normed, 1)

            def round_of_steps(r, first, last):
                for i in range(BACK):
                    if i + LEAD < BACK or not last:
                        tanh_out(r * BACK + i + LEAD)
                    normalise(r, i)

            for t in range(LEAD):
                tanh_out(t)
            rounds(act, round_of_steps)

        @block.vector
        def _(dve):
            def weight_lo(n):
                _, _, hi, lo, value, factor = pieces[n]
                dve.wait_ge(w_hi, n + 1)
                dve.scalar_tensor_tensor(lo, value, factor, hi.bitcast(F32), ALU.mult, ALU.subtract).then_inc(w_lo, 1)

            def step_lo(t, k):
                dve.wait_ge(xs_hi, t * 2 + k + 1)
                dve.tensor_tensor(xt_l[:, k, :], work[k][:, :], xt_h[:, k, :].bitcast(F32), ALU.subtract).then_inc(xs_lo, 1)

            def keep_hpre(t):
                dve.wait_ge(hp_full, t * 2 + 2)
                dve.tensor_copy(hpre[:, t, 2:4, :], work[1][:, :].rearrange("p (c n) -> p c n", c=2)).then_inc(hp_done, 1)

            def keep_state(t, k):
                dve.wait_ge(gate_done, t * 6 + 3 * k + 1)
                dve.scalar_tensor_tensor(keep[:, k, :], act_out[:, k, 0, :], 1.0, state[:, k, :], ALU.add, ALU.mult).then_inc(kept, 1)

            def add_gain(t, k):
                dve.wait_ge(gate_done, t * 6 + 3 * k + 3)
                dve.scalar_tensor_tensor(gain[:, k, :], act_out[:, k, 1, :], 1.0, act_out[:, k, 2, :], ALU.add, ALU.mult).then_inc(gained, 1)
                dve.wait_ge(kept, t * 2 + k + 1)
                dve.wait_ge(gained, t * 2 + k + 1)
                dve.scalar_tensor_tensor(state[:, k, :], keep[:, k, :], 0.5, gain[:, k, :], ALU.mult, ALU.add).then_inc(s_done, 1)

            def state_lo(t, k):
                dve.wait_ge(s_hi, t * 2 + k + 1)
                dve.tensor_tensor(s_l[:, k, :], state[:, k, :], s_h[:, k, :].bitcast(F32), ALU.subtract).then_inc(s_lo, 1)

            dve.wait_ge(shared.params_in, 3 * 16)
            dve.memset(gain[:, 0, :], 2.0).then_inc(state_set, 1)
            dve.tensor_scalar(bias[:, 0:2, :], bias_in[:, 0:2, :], 0.5, None, ALU.mult).then_inc(biased, 1)
            dve.tensor_copy(bias[:, 2, :], bias_in[:, 2, :]).then_inc(biased, 1)
            step_lo(0, 0)
            step_lo(0, 1)
            weight_lo(0)
            weight_lo(1)
            keep_hpre(0)
            dve.wait_ge(state_set, 1)
            for k in range(KC):
                dve.tensor_scalar(state[:, k, :], gain[:, 0, :], shared.c_in[:, k:k + 1], None, ALU.mult).then_inc(state_set, 1)
            dve.wait_ge(state_set, 1 + KC)
            dve.tensor_copy(s_h[:, :, :], state[:, :, :]).then_inc(state_hi_set, 1)
            dve.wait_ge(state_hi_set, 1)
            for k in range(KC):
                dve.tensor_tensor(s_l[:, k, :], state[:, k, :], s_h[:, k, :].bitcast(F32), ALU.subtract).then_inc(s_lo, 1)
            weight_lo(2)
            weight_lo(3)
            step_lo(1, 0)
            step_lo(1, 1)

            def step(t, more, further):
                keep_state(t, 0)
                add_gain(t, 0)
                keep_state(t, 1)
                state_lo(t, 0)
                add_gain(t, 1)
                state_lo(t, 1)
                if more:
                    keep_hpre(t + 1)
                if further:
                    step_lo(t + 2, 0)
                    step_lo(t + 2, 1)

            with dve.Fori(0, T - 2) as t:
                step(t, True, True)
            step(T - 2, True, False)
            step(T - 1, False, False)
            for i in range(2):
                dve.wait_ge(co_full, i + 1)
                dve.tensor_copy(c_out[:, 2 * i:2 * i + 2, :], work[i][:, :].rearrange("p (c n) -> p c n", c=2)).then_inc(co_done, 1)
            dve.wait_ge(co_done, 2)
            dve.tensor_tensor(c_out[:, :, :], c_out[:, :, :], shared.bo_row[:, :].unsqueeze(1).to_broadcast([P, TC, H]), ALU.add).then_inc(co_done, 1)
            dve.wait_ge(co_done, 3)
            dve.wait_ge(hp_done, 2 * T)

            def add_state(t):
                dve.tensor_tensor(hpre[:, t, 0, :], hpre[:, t, 0, :], c_out[:, 0, :], ALU.add).then_inc(dve_added, 1)

            def add_x(r, i, first):
                t = r * BACK + i
                dve.wait_ge(tanh_done, t + 1)
                dve.wait_ge(in_back[i], r * 16 + 16)
                if not first:
                    dve.wait_ge(stored[i], r * 16)
                dve.tensor_tensor(summed[:, i, :, :], x_back[:, i, :, :], hpre[:, t, :, :], ALU.add).then_inc(sum_done, 1)

            def round_of_steps(r, first, last):
                for i in range(BACK):
                    t = r * BACK + i
                    dve.wait_ge(sum_done, t + 1)
                    for c in range(TC):
                        dve.bn_stats(stats[:, i, c, :], summed[:, i, c, :]).then_inc(bn_done, 1)
                    if i + 1 < BACK:
                        add_x(r, i + 1, first)
                    elif not last:
                        add_x(r + 1, 0, False)
                    if i + LEAD < BACK or not last:
                        add_state(t + LEAD)
                    if not first:
                        dve.wait_ge(ln_step, t * 4 - (BACK - 1) * 4 + 3)
                    dve.wait_ge(bn_done, t * TC + TC)
                    dve.memset(fence[:, :], 0.0)
                    for c in range(TC):
                        dve.bn_aggr(mv[:, i, c, :], stats[:, i, c, :]).then_inc(mv_done, 1)

            for t in range(LEAD):
                add_state(t)
            add_x(0, 0, True)
            rounds(dve, round_of_steps)

        @block.tensor
        def _(pe):
            parts = [(0, 0), (1, 0), (0, 1)]

            def transpose_step(t, first):
                pe.wait_ge(x_in, t * 16 + 16)
                for k in range(KC):
                    if not first:
                        pe.wait_ge(hp_done, t * 2)
                    for c in range(TC):
                        last = pe.transpose(work[k][:, P * c:P * c + P], x_step[:, c, P * k:P * k + P], id_sb[:, :])
                    last.then_inc(xs_full, 1)

            def tokens_by(i, lhs, w, done):
                for j in range(2):
                    c = 2 * i + j
                    terms = [(k, a, d) for k in range(KC) for a, d in parts]
                    for m, (k, a, d) in enumerate(terms):
                        last = pe.matmul(work[i][:, H * j:H * j + H], lhs[a][:, k, P * c:P * c + P], (wo_h, wo_l)[d][:, w, k, :],
                                         start=(m == 0), stop=(m == len(terms) - 1))
                last.then_inc(done, 1)

            def gates_of(n, k, lhs, rhs, start, stop):
                g, mc = n % GATES, n // GATES
                for m, (a, d) in enumerate(parts):
                    last = pe.matmul(gate_ps[n][:, :], lhs[a][:, g, k, P * mc:P * mc + P], rhs[d][:, k, :],
                                     start=start and m == 0, stop=stop and m == len(parts) - 1)
                return last

            def from_x(t, first):
                pe.wait_ge(xs_lo, t * 2 + 2)
                if first:
                    pe.wait_ge(w_lo, 1)
                for i in range(2):
                    tokens_by(i, (xt_h, xt_l), 0, hp_full)
                if first:
                    pe.wait_ge(w_lo, 2)
                for n in range(GATES * KC):
                    if not first:
                        pe.wait_ge(gate_done, t * 6 - 5 + n)
                    for k in range(KC):
                        gates_of(n, k, (wx_h, wx_l), (xt_h, xt_l), k == 0, False)

            def from_state(t):
                for k in range(KC):
                    pe.wait_ge(s_lo, t * 2 + k + 1)
                    for n in range(GATES * KC):
                        last = gates_of(n, k, (uc_h, uc_l), (s_h, s_l), False, k == KC - 1)
                        if k == KC - 1:
                            last.then_inc(gate_full, 1)

            transpose_step(0, True)
            from_x(0, True)
            transpose_step(1, False)
            pe.wait_ge(w_lo, 3)
            with pe.Fori(0, T - 2) as t:
                from_state(t)
                from_x(t + 1, False)
                transpose_step(t + 2, False)
            from_state(T - 2)
            from_x(T - 1, False)
            from_state(T - 1)
            pe.wait_ge(s_lo, 2 * T + 2)
            pe.wait_ge(hp_done, 2 * T)
            pe.wait_ge(w_lo, 4)
            for i in range(2):
                tokens_by(i, (s_h, s_l), 1, co_full)


def build(nc, x, Wq, Wkv_short, Wkv_long, Wo, mix, decay, wx, uc, gate_bias, wo, uo, bo, in_c,
          ident, absdiff, qrows, krows, kab, out):
    x1 = nc.dram_tensor("x1_dram", [B, L, H], F32, kind="Internal").ap()
    with ExitStack() as ctx:
        shared = Shared(nc, ctx)
        attention_phase(nc, shared, x, x1, Wq, Wkv_short, Wkv_long, Wo, mix, decay, wx, uc, gate_bias, wo, uo, bo, in_c,
                        ident, absdiff, qrows, krows, kab)
        recurrence_phase(nc, shared, x1, out)


def constants():
    import numpy as np

    pos = np.arange(L, dtype=np.float32)
    chunk = np.arange(L) // P
    rows = ROWS - BIAS_ROW
    q = np.zeros((rows, 2, L), np.float32)
    k = np.zeros((rows, L), np.float32)
    kab = np.zeros((rows, 4), np.float32)
    for c in range(TC):
        sign, own = np.sign(chunk - c).astype(np.float32), (chunk == c).astype(np.float32)
        q[4 * c], q[4 * c + 1], q[4 * c + 2], q[4 * c + 3] = (t for t in (sign * pos, sign * pos, sign, sign))
        q[4 * c:4 * c + 4, 1] = 0
        k[4 * c:4 * c + 2], k[4 * c + 2:4 * c + 4] = -own, own * pos
    kab[:4 * TC, 0] = 1
    kab[4 * TC:, 1] = 1
    kab[1:4 * TC:2, 2] = -1
    q[MAX_ROW - BIAS_ROW, 1] = 1
    k[MAX_ROW - BIAS_ROW + 1] = 1
    q[MAX_ROW - BIAS_ROW:, 0] = 0
    return {"ident": np.eye(P, dtype=np.float32), "absdiff": np.abs(np.arange(P)[:, None] - np.arange(P)).astype(np.float32),
            "qrows": q.reshape(rows, 2 * L), "krows": k, "kab": kab}


def kernel(**inputs):
    import numpy as np
    import concourse.bacc as bacc
    from concourse.bass_utils import run_bass_kernel_spmd

    own = {k.removeprefix("L0_"): np.asarray(v) for k, v in inputs.items()}
    by_partition = lambda a: np.moveaxis(a.reshape(*a.shape[:-1], KC, P), -1, 0)
    t = lambda n: np.ascontiguousarray(own[n].T)
    arrays = {
        "x": own["attn_x"], "Wq": own["attn_Wq"], "Wkv_short": own["attn_Wkv_short"], "Wkv_long": own["attn_Wkv_long"],
        "Wo": own["attn_Wo"], "mix": own["attn_mix_weight"].reshape(1), "decay": own["attn_decay_factor"].reshape(1),
        "wx": np.stack([t("ffn_wf"), t("ffn_wi"), t("ffn_wc")]), "uc": np.stack([t("ffn_uf"), t("ffn_ui"), t("ffn_uc")]),
        "gate_bias": by_partition(np.stack([own["ffn_bf"], own["ffn_bi"], own["ffn_bc"]])),
        "wo": t("ffn_wo"), "uo": t("ffn_uo"), "bo": own["ffn_bo"], "in_c": by_partition(own["ffn_in_c"]),
    } | constants()
    arrays = {f"in_{k}": np.ascontiguousarray(v) for k, v in arrays.items()}
    nc = bacc.Bacc("TRN2", target_bir_lowering=False, num_devices=1)
    args = [nc.dram_tensor(k, v.shape, mybir.dt.from_np(v.dtype), kind="ExternalInput").ap() for k, v in arrays.items()]
    out = nc.dram_tensor("out", (B, L, H), F32, kind="ExternalOutput").ap()
    build(nc, *args, out)
    result = run_bass_kernel_spmd(nc, [arrays], core_ids=[0])
    return result.results[0]["out"]
```

```python
import concourse.bass as bass
from concourse import mybir
from concourse.alu_op_type import AluOpType as ALU
from contextlib import ExitStack

F32 = mybir.dt.float32
F32R = mybir.dt.float32r
ACT = mybir.ActivationFunctionType

B, L, H = 16, 512, 256
P = 128
NH = 16
HD = H // NH
TC = L // P
KC = H // P
GH = 4
GATES = 3
UNITS = 2 * NH // GH
SLOTS = UNITS * TC
RING = 4
AHEAD = 8
SCALE = 0.25
LEAD = 3
BACK = 4
EPS = 1e-5

BIAS_ROW = 3 * HD
ZERO_ROW = BIAS_ROW + 4 * TC
MAX_ROW = ZERO_ROW + 1
ROWS = MAX_ROW + 2
VW = HD + 1
VHALF = 8 * VW + HD - 1

TASKS = {0: ("v", 2, 0), 3: ("v", 3, 0), 4: ("ot", 0, -1), 7: ("ot", 1, -1), 8: ("xt", 0, 1), 11: ("xt", 1, 1),
         12: ("kq", 0, 1), 15: ("kq", 1, 1), 16: ("kq", 2, 1), 19: ("wo", 0, -1), 20: ("wo", 1, -1),
         23: ("v", 0, 1), 24: ("v", 1, 1), 27: ("kq", 3, 1), 28: ("kq", 4, 1), 31: ("kq", 5, 1),
         2: ("pvt", UNITS - 1, -1)}
TASKS |= {4 * u + 6: ("pvt", u, 0) for u in range(UNITS - 1)}
TASKS |= {4 * u - 3: ("shift", u, 0) for u in range(1, UNITS)} | {SLOTS - 3: ("shift", 0, 1)}
NORM_SLOT = 25
COUNT = {"v": 4, "ot": 2, "wo": 2, "xt": 2, "kq": 6, "pvt": UNITS, "shift": UNITS}


def exists(b):
    return not isinstance(b, int) or 0 <= b < B


def wait(eng, sem, b, per, k):
    value = b * per + k
    if isinstance(value, int) and value <= 0:
        return
    eng.wait_ge(sem, value)


def bodies(eng, body):
    body(-1)
    body(0)
    with eng.Fori(1, B - 1) as b:
        body(b)
    body(B - 1)
    body(B)


def unit_of(b, u):
    return (b, u) if u < UNITS else (b + 1, u - UNITS)


def attention_phase(nc, shared, x, x1, Wq, Wks, Wkl, Wo, mix, decay, wx, uc, gate_bias, wo, uo, bo, in_c, ident, absdiff, qrows, krows, kab):
    ctx = ExitStack()
    with ctx:
        sb = lambda n, s, d=F32: ctx.enter_context(nc.sbuf_tensor(n, s, d))
        pb = lambda n, s: ctx.enter_context(nc.psum_tensor(n, s, F32))
        sem = lambda n: ctx.enter_context(nc.semaphore(n))

        w_hi, w_lo = sb("w_hi", [P, 4, KC, H], F32R), sb("w_lo", [P, 4, KC, H], F32R)
        wv_hi, wv_lo = sb("wv_hi", [P, KC, 2, 2, P], F32R), sb("wv_lo", [P, KC, 2, 2, P], F32R)
        x_in, probs, id_sb, x1_stored = shared.x_step, shared.probs, shared.ident, shared.x1_stored
        x_res = sb("x_res", [P, TC, H])
        xt_h, xt_l = sb("xt_h", [P, KC, L], F32R), sb("xt_l", [P, KC, L], F32R)
        kq_h, kq_l = sb("kq_h", [P, 3, 2, L], F32R), sb("kq_l", [P, 3, 2, L], F32R)
        k_op = [sb(f"k_op{i}", [ROWS, GH, L], F32R) for i in range(RING)]
        q_op = [sb(f"q_op{i}", [ROWS, GH, L], F32R) for i in range(RING)]
        vals = sb("vals", [P, TC, 2, 2, VHALF])
        maxes, half_maxes = sb("maxes", [P, 2, GH, TC]), sb("half_maxes", [P, 2, GH, TC])
        shift_rows = sb("shift_rows", [GH * TC, 2, P], F32R)
        pv_sb = sb("pv_sb", [P, 2, L])
        rden, rdena = sb("rden", [P, 2, TC, GH]), sb("rdena", [P, 2, TC, GH])
        o_att = [sb(f"o_att{a}", [P, TC, NH, HD]) for a in range(2)]
        o_sum = sb("o_sum", [P, TC, H])
        ot_h, ot_l = sb("ot_h", [P, KC, L], F32R), sb("ot_l", [P, KC, L], F32R)
        res = sb("res", [P, TC, H])
        stats, mv = sb("stats", [P, TC, 6]), sb("mv", [P, TC, 2])
        veps, rstd, nmr = (sb(n, [P, TC]) for n in ("veps", "rstd", "nmr"))
        consts = sb("consts", [P, 3, TC])
        id_r = sb("id_r", [P, P], F32R)
        dist = sb("dist", [P, P])
        dist_h, dist_l = sb("dist_h", [P, P], F32R), sb("dist_l", [P, P], F32R)
        small = sb("small", [P, 8])
        kab_sb = sb("kab_sb", [ROWS - BIAS_ROW, 4])
        NR = ROWS - BIAS_ROW

        stage = probs[:, :, :, :].rearrange("p a h n -> p (a h n)")
        st_q = stage[:, 0:512].rearrange("p (k n) -> p k n", k=KC)
        st_kv = [stage[:, 512 + 1024 * a:1536 + 1024 * a].rearrange("p (k n) -> p k n", k=KC) for a in range(2)]
        st_o = stage[:, 2560:3072].rearrange("p (k n) -> p k n", k=KC)
        rows_in = o_sum[:, :, :].rearrange("p t n -> p (t n)")
        rows_tmp = res[:, :, :].rearrange("p t n -> p (t n)")
        rows_out = ot_h[:, :, :].rearrange("p k n -> p (k n)")
        rows_h = ot_l[:, :, :].rearrange("p k n -> p (k n)")

        b_ps = [pb(f"b_ps{i}", [P, 2, L]) for i in range(2)]
        a_ps = [pb(f"a_ps{i}", [P, L]) for i in range(2)]
        pv_ps = pb("pv_ps", [P, L])
        work = pb("work", [P, L])

        const_in, rows_set, setup, ones_set, exp_mix = map(sem, ("const_in", "rows_set", "setup", "ones_set", "exp_mix"))
        x_loaded, res_loaded = map(sem, ("x_loaded", "res_loaded"))
        k_loaded = [sem(f"k_loaded{i}") for i in range(RING)]
        q_loaded = [sem(f"q_loaded{i}") for i in range(RING)]
        shift_loaded = [sem(f"shift_loaded{i}") for i in range(2)]
        full = {n: sem(f"{n}_full") for n in COUNT}
        b_full, a_full, pv_full = map(sem, ("b_full", "a_full", "pv_full"))
        a_reduced, joined, exp_done, pv_copied = map(sem, ("a_reduced", "joined", "exp_done", "pv_copied"))
        xt_hi, kq_hi, ot_hi = map(sem, ("xt_hi", "kq_hi", "ot_hi"))
        rden_done, rdena_done, osum_done, bn_done, mv_done = map(sem, ("rden_done", "rdena_done", "osum_done", "bn_done", "mv_done"))
        ln_step, normed = map(sem, ("ln_step", "normed"))
        done = {n: sem(f"{n}_done") for n in COUNT}
        w_hi_done, w_lo_done, rows_made = map(sem, ("w_hi_done", "w_lo_done", "rows_made"))
        N_ROWS, N_SETUP = 7, 7
        weights = [(w_hi[:, 0, :, :], w_lo[:, 0, :, :], st_q)]
        weights += [(w_hi[:, 1 + a, :, :], w_lo[:, 1 + a, :, :], st_kv[a][:, :, 0:H]) for a in range(2)]
        weights += [(wv_hi[:, k, :, a, :], wv_lo[:, k, :, a, :], st_kv[a][:, k, H:2 * H].rearrange("p (f n) -> p f n", f=2))
                    for a in range(2) for k in range(KC)]
        weights += [(w_hi[:, 3, :, :], w_lo[:, 3, :, :], st_o)]

        block = ctx.enter_context(nc.Block())

        @block.sync
        def _(sp):
            copy_words = lambda dst, src: sp.dma_start(dst.bitcast(F32), src.bitcast(F32))
            for dst, src in ((st_q, Wq.rearrange("(k p) n -> p k n", p=P)), (st_kv[0], Wkl.rearrange("(k p) n -> p k n", p=P)),
                             (st_kv[1], Wks.rearrange("(k p) n -> p k n", p=P)), (st_o, Wo.rearrange("(k p) n -> p k n", p=P)),
                             (id_sb[:, :], ident), (dist[:, :], absdiff),
                             (rows_in[0:NR, 0:L], krows), (rows_tmp[0:NR, 0:2 * L], qrows), (kab_sb[:, :], kab),
                             (small[:, 0:1], mix.unsqueeze(0).to_broadcast([P, 1])), (small[:, 1:2], decay.unsqueeze(0).to_broadcast([P, 1]))):
                sp.dma_start(dst, src).then_inc(const_in, 16)
            sp.wait_ge(rows_made, N_ROWS)
            for i in range(RING):
                copy_words(q_op[i][BIAS_ROW:MAX_ROW, :, :],
                           rows_h[0:NR - 2, 0:L].unsqueeze(1).to_broadcast([NR - 2, GH, L])).then_inc(rows_set, 16)
                copy_words(k_op[i][BIAS_ROW:ROWS, :, :],
                           rows_out[0:NR, (1 - i % 2) * L:(2 - i % 2) * L].unsqueeze(1).to_broadcast([NR, GH, L])).then_inc(rows_set, 16)

            def load_rows(dst, h, part, half, pos, order, s):
                at = pos + HD * h
                for r, src in enumerate(order):
                    copy_words(dst[HD * r:HD * r + HD, h, :], src[at:at + HD, part, half, :]).then_inc(s, 16)

            def projected(b, n):
                if isinstance(b, int):
                    wait(sp, done["kq"], b, 6, n)

            def load_k(b, u, h):
                if exists(b):
                    g, att = u // 2, u % 2
                    if h == 0:
                        projected(b, 3 * (g // 2) + 2 * att + 1)
                        wait(sp, b_full, b, 2 * SLOTS, 8 * (u - RING + 1))
                    load_rows(k_op[u % RING], h, 2 * att, g // 2, 64 * (g % 2), (kq_h, kq_l, kq_h), k_loaded[u % RING])

            def load_q(b, g, h):
                if exists(b):
                    if h == 0:
                        projected(b, 3 * (g // 2) + 2)
                        wait(sp, b_full, b, 2 * SLOTS, 2 * (8 * g - 14))
                    load_rows(q_op[g], h, 1, g // 2, 64 * (g % 2), (kq_h, kq_h, kq_l), q_loaded[g])

            def body(b):
                for s in range(SLOTS):
                    first = isinstance(b, int) and b == -1
                    if s % 4 == 0 and not (first and s == 20) or first and s == 18:
                        for h in range(GH):
                            load_k(*unit_of(b, (s + 3) // 4 + 3), h)
                    if s % 8 == 2:
                        bb, u = unit_of(b, (s + 14) // 4)
                        for h in range(GH):
                            load_q(bb, u // 2, h)
                    if s in TASKS and TASKS[s][0] == "shift":
                        _, u, off = TASKS[s]
                        bb = b + off
                        if exists(bb):
                            wait(sp, done["shift"], bb, UNITS, u + 1)
                            copy_words(q_op[u // 2][MAX_ROW + u % 2:MAX_ROW + u % 2 + 1, :, :].rearrange("r h (t n) -> r (h t) n", n=P),
                                       shift_rows[:, u % 2, :]).then_inc(shift_loaded[u % 2], 16)

            bodies(sp, body)
            sp.wait_ge(full["xt"], 2 * B)
            sp.wait_ge(x1_stored, 16 + 16 * (B - 1))
            sp.dma_start(x_in[:, :, :], x1[0].rearrange("(c p) n -> p c n", p=P)).then_inc(shared.x_in, 16)
            sp.wait_ge(pv_full, B * SLOTS)
            for g, w in enumerate((wo, uo)):
                sp.dma_start(shared.stage_o[:, g, :, :], w.rearrange("(k p) n -> p k n", p=P)).then_inc(shared.output_in, 16)
            for g in range(GATES):
                sp.dma_start(shared.stage_w[:, g, :, :], wx[g].rearrange("(k p) n -> p k n", p=P)).then_inc(shared.wx_in, 16)
            for g in range(GATES):
                sp.dma_start(shared.stage_u[:, g, :, :], uc[g].rearrange("(k p) n -> p k n", p=P)).then_inc(shared.uc_in, 16)
            sp.dma_start(shared.bias_in[:, :, :], gate_bias).then_inc(shared.params_in, 16)
            sp.dma_start(shared.c_in[:, :], in_c).then_inc(shared.params_in, 16)
            sp.dma_start(shared.bo_row[:, :], bo.unsqueeze(0).to_broadcast([P, H])).then_inc(shared.params_in, 16)

        @block.gpsimd
        def _(pool):
            for n, value in ((0, EPS), (1, -0.5), (2, -1.0)):
                pool.memset(consts[:, n, :], value).then_inc(ln_step, 1)
            pool.wait_ge(ln_step, 3)
            pool.memset(nmr[:, :], 0.0).then_inc(x1_stored, 16)

            def body(b):
                bb = b - 1
                if exists(bb):
                    wait(pool, done["pvt"], bb, UNITS, UNITS)
                    pool.tensor_tensor(o_sum[:, :, :], o_att[0][:, :, :, :].rearrange("p t h d -> p t (h d)"),
                                       o_att[1][:, :, :, :].rearrange("p t h d -> p t (h d)"), ALU.add).then_inc(osum_done, 1)
                    wait(pool, mv_done, bb, TC, TC)
                    pool.tensor_tensor(veps[:, :], mv[:, :, 1], consts[:, 0, :], ALU.add).then_inc(ln_step, 1)
                    wait(pool, ln_step, bb, 4, 3 + 1)
                    pool.tensor_tensor(rstd[:, :], veps[:, :], consts[:, 1, :], ALU.pow).then_inc(ln_step, 1)
                    pool.tensor_tensor(nmr[:, :], mv[:, :, 0], consts[:, 2, :], ALU.mult).then_inc(ln_step, 1)
                    wait(pool, ln_step, bb, 4, 3 + 3)
                    pool.tensor_tensor(nmr[:, :], nmr[:, :], rstd[:, :], ALU.mult).then_inc(ln_step, 1)

            bodies(pool, body)

        @block.scalar
        def _(act):
            act.dma_start(x_in[:, :, :], x[0].rearrange("(t p) n -> p t n", p=P)).then_inc(x_loaded, 16)
            act.wait_ge(const_in, 11 * 16)
            for hi, _, value in weights:
                act.activation(hi, value, ACT.Copy).then_inc(w_hi_done, 1)
            act.activation(small[:, 2:3], small[:, 0:1], ACT.Exp, scale=-1.0).then_inc(exp_mix, 1)

            def exp_pair(b, s, hp):
                wait(act, b_full, b, 2 * SLOTS, 2 * s + hp + 1)
                wait(act, pv_full, b, SLOTS, s - 1)
                dst, src = probs[:, s % 2, 2 * hp:2 * hp + 2, :], b_ps[hp][:, :, :]
                if s // 4 % 2:
                    dst, src = dst.rearrange("p h (f n) -> p h f n", f=2), src.rearrange("p f (h n) -> p h f n", h=2)
                act.activation(dst, src, ACT.Exp).then_inc(exp_done, 1)

            def part_or_values(b, s):
                if s not in TASKS or not exists(b + TASKS[s][2]):
                    return
                kind, n, off = TASKS[s]
                bb = b + off
                if kind in ("xt", "kq", "ot"):
                    dst, ready, scale = {"xt": (xt_h[:, n % 2, :], xt_hi, 1.0), "ot": (ot_h[:, n % 2, :], ot_hi, 1.0),
                                         "kq": (kq_h[:, n % 3, n // 3, :], kq_hi, SCALE if n % 3 == 1 else 1.0)}[kind]
                    wait(act, full[kind], bb, COUNT[kind], n + 1)
                    act.activation(dst, work[:, :], ACT.Copy, scale=scale).then_inc(ready, 1)
                if kind == "v":
                    wait(act, full["v"], bb, 4, n + 1)
                    if n == 2:
                        wait(act, pv_full, bb, SLOTS, 0)
                    for j in range(2):
                        src = work[:, 256 * j:256 * j + 256].rearrange("p (a h d) -> p a h d", a=2, d=HD)
                        dst = vals[:, 2 * (n % 2) + j, n // 2, :, 0:8 * VW].rearrange("p a (h e) -> p a h e", e=VW)[:, :, :, 0:HD]
                        act.activation(dst, src, ACT.Copy).then_inc(done["v"], 1)

            def body(b):
                for s in range(SLOTS):
                    if s == 1 and exists(b) and exists(b + 1):
                        act.dma_start(x_in[:, :, :], x[b + 1].rearrange("(t p) n -> p t n", p=P)).then_inc(x_loaded, 16)
                    if s == 21 and exists(b):
                        wait(act, done["wo"], b, 2, 0)
                        act.dma_start(x_res[:, :, :], x[b].rearrange("(t p) n -> p t n", p=P)).then_inc(res_loaded, 16)
                    if exists(b):
                        exp_pair(b, s, 0)
                        exp_pair(b, s, 1)
                    if 0 <= s - NORM_SLOT < TC and exists(b - 1):
                        t = s - NORM_SLOT
                        wait(act, ln_step, b - 1, 4, 3 + 4)
                        act.activation(res[:, t, :], res[:, t, :], ACT.Identity, bias=nmr[:, t:t + 1],
                                       scale=rstd[:, t:t + 1]).then_inc(normed, 1)
                        if t == TC - 1:
                            wait(act, normed, b - 1, TC, TC)
                            act.dma_start(x1[b - 1].rearrange("(t p) n -> p t n", p=P), res[:, :, :]).then_inc(x1_stored, 16)
                    part_or_values(b, s)
                    if s % 4 == 0:
                        bb, u = (b, s // 4 - 1) if s else (b - 1, UNITS - 1)
                        if exists(bb):
                            wait(act, pv_full, bb, SLOTS, 4 * u + 4)
                            act.activation(pv_sb[:, u % 2, :], pv_ps[:, :], ACT.Copy).then_inc(pv_copied, 1)

            bodies(act, body)

        @block.vector
        def _(dve):
            made = [0, 0]

            def row_step(*instructions):
                for i in instructions:
                    i.then_inc(rows_made, 1)
                made[0] += len(instructions)
                dve.wait_ge(rows_made, made[0])

            def setup_step(*instructions):
                for i in instructions:
                    i.then_inc(setup, 1)
                made[1] += len(instructions)
                dve.wait_ge(setup, made[1])

            def rows_of_bias():
                row_step(dve.tensor_scalar(small[:, 6:7], small[:, 1:2], -1.0, 1.0, ALU.mult, ALU.add),
                         dve.tensor_copy(rows_out[0:NR, L:2 * L], rows_tmp[0:NR, L:2 * L]),
                         dve.tensor_copy(rows_h[0:NR, 0:L], rows_tmp[0:NR, 0:L]))
                row_step(dve.tensor_scalar(kab_sb[:, 3:4], kab_sb[:, 0:1], small[0:NR, 6:7], kab_sb[:, 1:2], ALU.mult, ALU.add))
                row_step(dve.tensor_scalar(rows_in[0:NR, L:2 * L], rows_in[0:NR, 0:L], kab_sb[:, 3:4], None, ALU.mult))
                row_step(dve.tensor_copy(rows_h[0:NR, L:2 * L], rows_in[0:NR, L:2 * L]))
                row_step(dve.scalar_tensor_tensor(rows_out[0:NR, 0:L], rows_h[0:NR, L:2 * L].bitcast(F32), kab_sb[:, 2:3],
                                                  rows_in[0:NR, L:2 * L], ALU.mult, ALU.add))
                assert made[0] == N_ROWS

            def diagonal_bias():
                setup_step(dve.tensor_scalar(dist[:, :], dist[:, :], small[:, 6:7], -1.0, ALU.mult, ALU.mult),
                           dve.tensor_copy(id_r[:, :], id_sb[:, :]),
                           dve.tensor_scalar(small[:, 3:4], small[:, 2:3], 1.0, None, ALU.add))
                setup_step(dve.tensor_copy(dist_h[:, :], dist[:, :]),
                           dve.reciprocal(small[:, 5:6], small[:, 3:4]))
                setup_step(dve.tensor_tensor(dist_l[:, :], dist[:, :], dist_h[:, :].bitcast(F32), ALU.subtract),
                           dve.tensor_scalar(small[:, 4:5], small[:, 5:6], -1.0, 1.0, ALU.mult, ALU.add))
                assert made[1] == N_SETUP

            dve.memset(vals[:, :, :, :, :], 1.0).then_inc(ones_set, 1)

            def weights_rest(pieces):
                for n in pieces:
                    hi, lo, value = weights[n]
                    dve.wait_ge(w_hi_done, n + 1)
                    dve.tensor_tensor(lo, value, hi.bitcast(F32), ALU.subtract).then_inc(w_lo_done, 1)

            weights_rest(range(3))

            def rest(dst, hi, sem_hi, kind, bb, n, scale):
                wait(dve, sem_hi, bb, COUNT[kind], n + 1)
                dve.scalar_tensor_tensor(dst, work[:, :], scale, hi.bitcast(F32), ALU.mult, ALU.subtract).then_inc(done[kind], 1)

            def body(b):
                for s in range(SLOTS):
                    if isinstance(b, int) and b == -1 and s == 12:
                        rows_of_bias()
                    if isinstance(b, int) and b == -1 and s == 13:
                        weights_rest(range(3, len(weights)))
                        dve.wait_ge(exp_mix, 1)
                        diagonal_bias()
                    if s == 22 and exists(b - 1):
                        wait(dve, bn_done, b - 1, TC, TC)
                    bb, u = unit_of(b, (s + AHEAD) // 4)
                    def reduce(h, bb=bb, u=u, s=s):
                        if exists(bb):
                            wait(dve, a_full, bb, 16 * UNITS, 16 * u + 4 * (s % 4) + h + 1)
                            if u % 2:
                                if s % 4 == 0 and h == 0:
                                    wait(dve, joined, bb, UNITS // 2, u // 2)
                                dve.reduce_max(half_maxes[:, h % 2, 2 * (h // 2):2 * (h // 2) + 2, s % 4],
                                               a_ps[h % 2][:, :].rearrange("p (h n) -> p h n", h=2),
                                               mybir.AxisListType.X).then_inc(a_reduced, 1)
                            else:
                                dve.reduce_max(maxes[:, 0, h, s % 4:s % 4 + 1], a_ps[h % 2][:, :],
                                               mybir.AxisListType.X).then_inc(a_reduced, 1)

                    if s % 8 == 0 and exists(b):
                        n = s // 4 + 1
                        wait(dve, a_reduced, b, 16 * UNITS, 16 * n + 16)
                        wait(dve, full["shift"], b, UNITS, n - 1)
                        dve.tensor_tensor(maxes[:, 1, :, :], half_maxes[:, 0, :, :], half_maxes[:, 1, :, :], ALU.max).then_inc(joined, 1)

                    before = 2 if s in TASKS and TASKS[s][0] == "pvt" else 3
                    for h in range(before):
                        reduce(h)
                    if s in TASKS and exists(b + TASKS[s][2]):
                        kind, n, off = TASKS[s]
                        bb = b + off
                        if kind == "xt":
                            rest(xt_l[:, n, :], xt_h[:, n, :], xt_hi, kind, bb, n, 1.0)
                        if kind == "kq":
                            rest(kq_l[:, n % 3, n // 3, :], kq_h[:, n % 3, n // 3, :], kq_hi, kind, bb, n, SCALE if n % 3 == 1 else 1.0)
                        if kind == "ot":
                            rest(ot_l[:, n, :], ot_h[:, n, :], ot_hi, kind, bb, n, 1.0)
                        if kind == "shift":
                            wait(dve, full["shift"], bb, UNITS, n + 1)
                            wait(dve, shift_loaded[n % 2], bb, 16 * UNITS // 2, 16 * (n // 2))
                            dve.tensor_scalar(shift_rows[:, n % 2, :], work[0:GH * TC, 0:P], -1.0, None, ALU.mult).then_inc(done["shift"], 1)
                        if kind == "pvt":
                            g, att = n // 2, n % 2
                            o = work[:, :].rearrange("p (t h e) -> p t h e", t=TC, h=GH)
                            wait(dve, full["pvt"], bb, UNITS, n + 1)
                            dve.reciprocal(rden[:, att, :, :], o[:, :, :, HD]).then_inc(rden_done, 1)
                            wait(dve, rden_done, bb, UNITS, n + 1)
                            dve.tensor_scalar(rdena[:, att, :, :], rden[:, att, :, :], small[:, 4 + att:5 + att], None,
                                              ALU.mult).then_inc(rdena_done, 1)
                            wait(dve, rdena_done, bb, UNITS, n + 1)
                            if n < 2:
                                wait(dve, osum_done, bb, 1, 0)
                            dve.tensor_tensor(o_att[att][:, :, GH * g:GH * g + GH, :], o[:, :, :, 0:HD],
                                              rdena[:, att, :, :].unsqueeze(3).to_broadcast([P, TC, GH, HD]),
                                              ALU.mult).then_inc(done["pvt"], 1)
                        if kind == "wo":
                            wait(dve, full["wo"], bb, 2, n + 1)
                            wait(dve, res_loaded, bb, 16, 16)
                            wait(dve, x1_stored, bb, 16, 16)
                            r = res[:, 2 * n:2 * n + 2, :]
                            dve.tensor_tensor(r, work[:, :].rearrange("p (t n) -> p t n", t=2), x_res[:, 2 * n:2 * n + 2, :],
                                              ALU.add).then_inc(done["wo"], 1)
                            wait(dve, done["wo"], bb, 2, n + 1)
                            for j in range(2):
                                dve.bn_stats(stats[:, 2 * n + j, :], res[:, 2 * n + j, :]).then_inc(bn_done, 1)
                    for h in range(before, GH):
                        reduce(h)
                    if s == 22 and exists(b - 1):
                        for t in range(TC):
                            dve.bn_aggr(mv[:, t, :], stats[:, t, :]).then_inc(mv_done, 1)

            bodies(dve, body)

        @block.tensor
        def _(pe):
            pe.wait_ge(const_in, 11 * 16)

            def three(out, lhs, rhs):
                last = None
                pairs = [(k, a, c) for k in range(KC) for a, c in ((0, 0), (1, 0), (0, 1))]
                for i, (k, a, c) in enumerate(pairs):
                    last = pe.matmul(out, lhs(a, k), rhs(c, k), start=(i == 0), stop=(i == len(pairs) - 1))
                return last

            def score_half(bank, half, lhs, rhs, heads, chunk, rows, diagonals):
                diagonals = diagonals if chunk // 2 == half else ()
                for j, h in enumerate(heads):
                    last = pe.matmul(bank[:, 256 * j:256 * j + 256], lhs[0:rows, h, P * chunk:P * chunk + P],
                                     rhs[0:rows, h, 256 * half:256 * half + 256], start=(j == 0), stop=(j == 1 and not diagonals))
                blocks = bank.rearrange("p (h n) -> p h n", h=2)[:, :, P * (chunk % 2):P * (chunk % 2) + P]
                for i, d in enumerate(diagonals):
                    last = pe.matmul(blocks, id_r[:, :], d[:, :].unsqueeze(1).to_broadcast([P, 2, P]), start=False,
                                     stop=(i == len(diagonals) - 1))
                return last

            def score_pair(b, s, hp):
                u, c = s // 4, s % 4
                q, k = q_op[u // 2], k_op[u % RING]
                if c == 0 and hp == 0:
                    wait(pe, shift_loaded[u % 2], b, 16 * UNITS // 2, 16 * (u // 2 + 1))
                wait(pe, exp_done, b, 2 * SLOTS, 2 * s + hp - 1)
                for j in range(2):
                    if u % 2:
                        last = score_half(b_ps[hp][:, j, :], j, k, q, (2 * hp, 2 * hp + 1), c, MAX_ROW + 2, (dist_h, dist_l))
                    else:
                        h = 2 * hp + j
                        last = pe.matmul(b_ps[hp][:, j, :], k[0:MAX_ROW + 1, h, P * c:P * c + P], q[0:MAX_ROW + 1, h, :],
                                         start=True, stop=True)
                last.then_inc(b_full, 1)

            def score_for_max(b, s, h):
                bb, u = unit_of(b, (s + AHEAD) // 4)
                c = s % 4
                if not exists(bb):
                    return
                q, k = q_op[u // 2], k_op[u % RING]
                if c == 0 and h == 0:
                    wait(pe, k_loaded[u % RING], bb, 384, 192 * (u // RING + 1))
                    wait(pe, q_loaded[u // 2], bb, 192, 192)
                    if isinstance(bb, int) and bb == 0 and u == 0:
                        pe.wait_ge(rows_set, 16 * 2 * RING)
                        pe.wait_ge(setup, N_SETUP)
                        pe.wait_ge(ones_set, 1)
                wait(pe, a_reduced, bb, 16 * UNITS, 16 * u + 4 * c + h - 1)
                if u % 2:
                    pair = 2 * (h // 2)
                    last = score_half(a_ps[h % 2][:, :], h % 2, q, k, (pair, pair + 1), c, MAX_ROW, (dist_h,))
                else:
                    last = pe.matmul(a_ps[h % 2][:, :], q[0:MAX_ROW, h, P * c:P * c + P], k[0:MAX_ROW, h, :], start=True, stop=True)
                last.then_inc(a_full, 1)

            def weigh(b, s):
                u, c = s // 4, s % 4
                g, att = u // 2, u % 2
                wait(pe, exp_done, b, 2 * SLOTS, 2 * s + 2)
                if c == 0:
                    wait(pe, pv_copied, b, UNITS, u)
                    if u in (0, UNITS // 2):
                        wait(pe, done["v"], b, 8, 4 if u == 0 else 8)
                for h in range(GH):
                    at = VW * (GH * (g % 2) + h)
                    last = pe.matmul(pv_ps[32 * h:32 * h + 32, :], vals[:, c, g // 2, att, at:at + 32], probs[:, s % 2, h, :],
                                     start=(c == 0), stop=(c == TC - 1))
                last.then_inc(pv_full, 1)

            def work_task(b, s):
                kind, n, off = TASKS[s]
                bb = b + off
                if not exists(bb):
                    return
                for back in range(1, SLOTS + 1):
                    at, ob = (s - back, b) if s >= back else (s - back + SLOTS, b - 1)
                    if isinstance(ob, int) and ob < -1:
                        break
                    if at in TASKS and exists(ob + TASKS[at][2]):
                        k0, n0, off0 = TASKS[at]
                        per, m = (8, 2 * n0 + 2) if k0 == "v" else (COUNT[k0], n0 + 1)
                        wait(pe, done[k0], ob + off0, per, m)
                        break
                if kind == "xt":
                    wait(pe, x_loaded, bb, 16, 16)
                    for t in range(TC):
                        last = pe.transpose(work[:, P * t:P * t + P], x_in[:, t, P * n:P * n + P], id_sb[:, :])
                if kind == "kq":
                    w, half = (1, 0, 2)[n % 3], n // 3
                    if isinstance(bb, int) and bb == 0 and n == 0:
                        pe.wait_ge(w_lo_done, 3)
                    wait(pe, done["xt"], bb, 2, 2)
                    last = three(work[:, :], lambda a, k: (w_hi, w_lo)[a][:, w, k, P * half:P * half + P],
                                 lambda a, k: (xt_h, xt_l)[a][:, k, :])
                if kind == "v":
                    wait(pe, done["xt"], bb, 2, 2)
                    if isinstance(bb, int) and bb == 0 and n == 0:
                        pe.wait_ge(w_lo_done, len(weights))
                    for j in range(2):
                        t = 2 * (n % 2) + j
                        last = three(work[:, 256 * j:256 * j + 256], lambda a, k: (xt_h, xt_l)[a][:, k, P * t:P * t + P],
                                     lambda a, k: (wv_hi, wv_lo)[a][:, k, n // 2, :, :])
                if kind == "ot":
                    wait(pe, osum_done, bb, 1, 1)
                    for t in range(TC):
                        last = pe.transpose(work[:, P * t:P * t + P], o_sum[:, t, P * n:P * n + P], id_sb[:, :])
                if kind == "wo":
                    wait(pe, done["ot"], bb, 2, 2)
                    for j in range(2):
                        t = 2 * n + j
                        last = three(work[:, 256 * j:256 * j + 256], lambda a, k: (ot_h, ot_l)[a][:, k, P * t:P * t + P],
                                     lambda a, k: (w_hi, w_lo)[a][:, 3, k, :])
                if kind == "pvt":
                    wait(pe, pv_copied, bb, UNITS, n + 1)
                    for t in range(TC):
                        last = pe.transpose(work[:, P * t:P * t + P], pv_sb[:, n % 2, P * t:P * t + P], id_sb[:, :])
                if kind == "shift":
                    if n % 2:
                        wait(pe, joined, bb, UNITS // 2, n // 2 + 1)
                    else:
                        wait(pe, a_reduced, bb, 16 * UNITS, 16 * n + 16)
                    last = pe.transpose(work[0:GH * TC, 0:P], maxes[:, n % 2, :, :].rearrange("p h t -> p (h t)"), id_sb[:, :])
                last.then_inc(full[kind], 1)

            def body(b):
                for s in range(SLOTS):
                    if exists(b):
                        score_pair(b, s, 0)
                    score_for_max(b, s, 0)
                    if exists(b):
                        score_pair(b, s, 1)
                    score_for_max(b, s, 1)
                    if s in TASKS:
                        work_task(b, s)
                    score_for_max(b, s, 2)
                    bb, ss = (b, s - 1) if s else (b - 1, SLOTS - 1)
                    if exists(bb):
                        weigh(bb, ss)
                    score_for_max(b, s, 3)

            bodies(pe, body)


class Shared:

    def __init__(self, nc, ctx):
        sb = lambda n, s: ctx.enter_context(nc.sbuf_tensor(n, s, F32))
        sem = lambda n: ctx.enter_context(nc.semaphore(n))
        self.ident = sb("ident_sb", [P, P])
        self.x_step = sb("x_step", [P, TC, H])
        self.bias_in, self.c_in, self.bo_row = sb("bias_in", [P, GATES, KC]), sb("c_in", [P, KC]), sb("bo_row", [P, H])
        self.probs = sb("probs", [P, 2, GH, L])
        stage = self.probs[:, :, :, :].rearrange("p a h n -> p (a h n)")
        self.stage_w = stage[:, 0:1536].rearrange("p (g k n) -> p g k n", g=GATES, k=KC)
        self.stage_u = stage[:, 1536:3072].rearrange("p (g k n) -> p g k n", g=GATES, k=KC)
        self.stage_o = stage[:, 3072:4096].rearrange("p (g k n) -> p g k n", g=2, k=KC)
        self.x1_stored, self.x_in, self.output_in, self.wx_in, self.uc_in, self.params_in = map(
            sem, ("x1_stored", "x_step_in", "output_in", "wx_in", "uc_in", "params_in"))


def recurrence_phase(nc, shared, x1, out):
    T = B
    ctx = ExitStack()
    with ctx:
        sb = lambda n, s, d=F32: ctx.enter_context(nc.sbuf_tensor(n, s, d))
        pb = lambda n, s: ctx.enter_context(nc.psum_tensor(n, s, F32))
        sem = lambda n: ctx.enter_context(nc.semaphore(n))

        wx_h, wx_l = sb("wx_h", [P, GATES, KC, H], F32R), sb("wx_l", [P, GATES, KC, H], F32R)
        uc_h, uc_l = sb("uc_h", [P, GATES, KC, H], F32R), sb("uc_l", [P, GATES, KC, H], F32R)
        wo_h, wo_l = sb("wo_h", [P, 2, KC, H], F32R), sb("wo_l", [P, 2, KC, H], F32R)
        hpre = sb("hpre", [P, T, TC, H])
        x_step, id_sb, x_in, bias_in = shared.x_step, shared.ident, shared.x_in, shared.bias_in
        xt_h, xt_l = sb("xs_h", [P, KC, L], F32R), sb("xs_l", [P, KC, L], F32R)
        act_out = sb("act_out", [P, KC, GATES, L])
        state, keep, gain = sb("state", [P, KC, L]), sb("keep", [P, KC, L]), sb("gain", [P, KC, L])
        s_h, s_l = sb("s_h", [P, KC, L], F32R), sb("s_l", [P, KC, L], F32R)
        bias, c_out = sb("bias", [P, GATES, KC]), sb("c_out", [P, TC, H])
        x_back, summed = sb("x_back", [P, BACK, TC, H]), sb("summed", [P, BACK, TC, H])
        stats, mv = sb("stats2", [P, BACK, TC, 6]), sb("mv2", [P, BACK, TC, 2])
        veps, rstd, nmr = (sb(n, [P, BACK, TC]) for n in ("veps2", "rstd2", "nmr2"))
        consts, fence = sb("consts2", [P, 3, TC]), sb("fence", [P, 1])

        gate_ps = [pb(f"gate_ps{i}", [P, L]) for i in range(GATES * KC)]
        work = [pb(f"work2_{i}", [P, L]) for i in range(2)]

        w_hi, w_lo, biased, state_set, state_hi_set, xs_full, xs_hi, xs_lo = map(sem, (
            "w2_hi_done", "w2_lo_done", "biased", "state_set", "state_hi_set", "xs_full", "xs_hi", "xs_lo"))
        hp_full, hp_done, gate_full, gate_done, kept, gained, s_done, s_hi, s_lo = map(sem, (
            "hp_full", "hp_done", "gate_full", "gate_done", "kept", "gained", "s_done", "s_hi_done", "s_lo_done"))
        co_full, co_done, pool_added, dve_added, tanh_done, sum_done, bn_done, mv_done, ln_step, normed = map(sem, (
            "co_full", "co_done", "pool_added", "dve_added", "tanh_done", "sum_done", "bn2_done", "mv2_done", "ln2_step", "normed2"))
        in_back = [sem(f"in_back{i}") for i in range(BACK)]
        stored = [sem(f"stored{i}") for i in range(BACK)]
        pieces = ((shared.output_in, 2, wo_h[:, 0, :, :], wo_l[:, 0, :, :], shared.stage_o[:, 0, :, :], 1.0),
                  (shared.wx_in, GATES, wx_h[:, :, :, :], wx_l[:, :, :, :], shared.stage_w, 1.0),
                  (shared.uc_in, GATES, uc_h[:, :, :, :], uc_l[:, :, :, :], shared.stage_u, 0.5),
                  (shared.output_in, 2, wo_h[:, 1, :, :], wo_l[:, 1, :, :], shared.stage_o[:, 1, :, :], 0.5))

        block = ctx.enter_context(nc.Block())
        tokens = lambda ap: ap.rearrange("(c p) n -> p c n", p=P)

        def rounds(eng, round_of_steps):
            round_of_steps(0, True, False)
            with eng.Fori(1, T // BACK - 1) as r:
                round_of_steps(r, False, False)
            round_of_steps(T // BACK - 1, False, True)

        @block.sync
        def _(sp):
            sp.wait_ge(shared.x1_stored, 16 + 16 * B)
            for t in range(BACK):
                sp.dma_start(x_back[:, t, :, :], tokens(x1[t])).then_inc(in_back[t], 16)
            for t in range(T):
                if t + BACK < T:
                    sp.wait_ge(sum_done, t + 1)
                    sp.dma_start(x_back[:, t % BACK, :, :], tokens(x1[t + BACK])).then_inc(in_back[t % BACK], 16)
                sp.wait_ge(normed, TC * (t + 1))
                sp.dma_start(tokens(out[t]), summed[:, t % BACK, :, :]).then_inc(stored[t % BACK], 16)
            for i in range(BACK):
                sp.wait_ge(stored[i], 16 * T // BACK)

        @block.gpsimd
        def _(pool):
            for n, value in ((0, EPS), (1, -0.5), (2, -1.0)):
                pool.memset(consts[:, n, :], value).then_inc(ln_step, 1)
            pool.wait_ge(ln_step, 3)
            pool.wait_ge(co_done, 2)
            pool.wait_ge(hp_done, 2 * T)

            def add_state(t):
                pool.tensor_tensor(hpre[:, t, 1:TC, :], hpre[:, t, 1:TC, :], c_out[:, 1:TC, :], ALU.add).then_inc(pool_added, 1)

            def scales(r, i, first):
                t = r * BACK + i
                if not first:
                    pool.wait_ge(normed, t * TC - (BACK - 1) * TC)
                pool.wait_ge(mv_done, t * TC + TC)
                pool.tensor_tensor(veps[:, i, :], mv[:, i, :, 1], consts[:, 0, :], ALU.add).then_inc(ln_step, 1)
                pool.wait_ge(ln_step, t * 4 + 3 + 1)
                pool.tensor_tensor(rstd[:, i, :], veps[:, i, :], consts[:, 1, :], ALU.pow).then_inc(ln_step, 1)
                pool.tensor_tensor(nmr[:, i, :], mv[:, i, :, 0], consts[:, 2, :], ALU.mult).then_inc(ln_step, 1)
                pool.wait_ge(ln_step, t * 4 + 3 + 3)
                pool.tensor_tensor(nmr[:, i, :], nmr[:, i, :], rstd[:, i, :], ALU.mult).then_inc(ln_step, 1)

            def round_of_steps(r, first, last):
                for i in range(BACK):
                    if i + LEAD < BACK or not last:
                        add_state(r * BACK + i + LEAD)
                    scales(r, i, first)

            for t in range(LEAD):
                add_state(t)
            rounds(pool, round_of_steps)

        @block.scalar
        def _(act):
            def weight_hi(n):
                loaded, loads, hi, _, value, factor = pieces[n]
                act.wait_ge(loaded, 16 * loads)
                act.activation(hi, value, ACT.Copy, scale=factor).then_inc(w_hi, 1)

            def gate(t, n):
                k, g = n // GATES, n % GATES
                act.wait_ge(gate_full, t * 6 + n + 1)
                act.activation(act_out[:, k, g, :], gate_ps[n][:, :], ACT.Tanh, bias=bias[:, g, k:k + 1],
                               scale=0.5 if g < 2 else 1.0).then_inc(gate_done, 1)

            def state_hi(t, k):
                act.wait_ge(s_done, t * 2 + k + 1)
                act.activation(s_h[:, k, :], state[:, k, :], ACT.Copy).then_inc(s_hi, 1)

            def step_hi(t, k):
                act.wait_ge(xs_full, t * 2 + k + 1)
                act.activation(xt_h[:, k, :], work[k][:, :], ACT.Copy).then_inc(xs_hi, 1)

            def keep_hpre(t):
                act.wait_ge(hp_full, t * 2 + 1)
                act.activation(hpre[:, t, 0:2, :], work[0][:, :].rearrange("p (c n) -> p c n", c=2), ACT.Copy).then_inc(hp_done, 1)

            def load_step(t):
                act.dma_start(x_step[:, :, :], tokens(x1[t])).then_inc(x_in, 16)

            act.wait_ge(shared.x1_stored, 16 + 16 * B)
            step_hi(0, 0)
            step_hi(0, 1)
            load_step(1)
            weight_hi(0)
            weight_hi(1)
            keep_hpre(0)
            weight_hi(2)
            weight_hi(3)
            step_hi(1, 0)
            step_hi(1, 1)
            load_step(2)
            act.wait_ge(biased, 2)

            def step(t, more, further, load):
                for n in range(5):
                    gate(t, n)
                state_hi(t, 0)
                gate(t, 5)
                state_hi(t, 1)
                if more:
                    keep_hpre(t + 1)
                if further:
                    step_hi(t + 2, 0)
                    step_hi(t + 2, 1)
                if load:
                    load_step(t + 3)

            with act.Fori(0, T - 3) as t:
                step(t, True, True, True)
            step(T - 3, True, True, False)
            step(T - 2, True, False, False)
            step(T - 1, False, False, False)

            def tanh_out(t):
                act.wait_ge(pool_added, t + 1)
                act.wait_ge(dve_added, t + 1)
                act.activation(hpre[:, t, :, :], hpre[:, t, :, :], ACT.Tanh).then_inc(tanh_done, 1)

            def normalise(r, i):
                t = r * BACK + i
                act.wait_ge(ln_step, t * 4 + 3 + 4)
                for c in range(TC):
                    act.activation(summed[:, i, c, :], summed[:, i, c, :], ACT.Identity, bias=nmr[:, i, c:c + 1],
                                   scale=rstd[:, i, c:c + 1]).then_inc(normed, 1)

            def round_of_steps(r, first, last):
                for i in range(BACK):
                    if i + LEAD < BACK or not last:
                        tanh_out(r * BACK + i + LEAD)
                    normalise(r, i)

            for t in range(LEAD):
                tanh_out(t)
            rounds(act, round_of_steps)

        @block.vector
        def _(dve):
            def weight_lo(n):
                _, _, hi, lo, value, factor = pieces[n]
                dve.wait_ge(w_hi, n + 1)
                dve.scalar_tensor_tensor(lo, value, factor, hi.bitcast(F32), ALU.mult, ALU.subtract).then_inc(w_lo, 1)

            def step_lo(t, k):
                dve.wait_ge(xs_hi, t * 2 + k + 1)
                dve.tensor_tensor(xt_l[:, k, :], work[k][:, :], xt_h[:, k, :].bitcast(F32), ALU.subtract).then_inc(xs_lo, 1)

            def keep_hpre(t):
                dve.wait_ge(hp_full, t * 2 + 2)
                dve.tensor_copy(hpre[:, t, 2:4, :], work[1][:, :].rearrange("p (c n) -> p c n", c=2)).then_inc(hp_done, 1)

            def keep_state(t, k):
                dve.wait_ge(gate_done, t * 6 + 3 * k + 1)
                dve.scalar_tensor_tensor(keep[:, k, :], act_out[:, k, 0, :], 1.0, state[:, k, :], ALU.add, ALU.mult).then_inc(kept, 1)

            def add_gain(t, k):
                dve.wait_ge(gate_done, t * 6 + 3 * k + 3)
                dve.scalar_tensor_tensor(gain[:, k, :], act_out[:, k, 1, :], 1.0, act_out[:, k, 2, :], ALU.add, ALU.mult).then_inc(gained, 1)
                dve.wait_ge(kept, t * 2 + k + 1)
                dve.wait_ge(gained, t * 2 + k + 1)
                dve.scalar_tensor_tensor(state[:, k, :], keep[:, k, :], 0.5, gain[:, k, :], ALU.mult, ALU.add).then_inc(s_done, 1)

            def state_lo(t, k):
                dve.wait_ge(s_hi, t * 2 + k + 1)
                dve.tensor_tensor(s_l[:, k, :], state[:, k, :], s_h[:, k, :].bitcast(F32), ALU.subtract).then_inc(s_lo, 1)

            dve.wait_ge(shared.params_in, 3 * 16)
            dve.memset(gain[:, 0, :], 2.0).then_inc(state_set, 1)
            dve.tensor_scalar(bias[:, 0:2, :], bias_in[:, 0:2, :], 0.5, None, ALU.mult).then_inc(biased, 1)
            dve.tensor_copy(bias[:, 2, :], bias_in[:, 2, :]).then_inc(biased, 1)
            step_lo(0, 0)
            step_lo(0, 1)
            weight_lo(0)
            weight_lo(1)
            keep_hpre(0)
            dve.wait_ge(state_set, 1)
            for k in range(KC):
                dve.tensor_scalar(state[:, k, :], gain[:, 0, :], shared.c_in[:, k:k + 1], None, ALU.mult).then_inc(state_set, 1)
            dve.wait_ge(state_set, 1 + KC)
            dve.tensor_copy(s_h[:, :, :], state[:, :, :]).then_inc(state_hi_set, 1)
            dve.wait_ge(state_hi_set, 1)
            for k in range(KC):
                dve.tensor_tensor(s_l[:, k, :], state[:, k, :], s_h[:, k, :].bitcast(F32), ALU.subtract).then_inc(s_lo, 1)
            weight_lo(2)
            weight_lo(3)
            step_lo(1, 0)
            step_lo(1, 1)

            def step(t, more, further):
                keep_state(t, 0)
                add_gain(t, 0)
                keep_state(t, 1)
                state_lo(t, 0)
                add_gain(t, 1)
                state_lo(t, 1)
                if more:
                    keep_hpre(t + 1)
                if further:
                    step_lo(t + 2, 0)
                    step_lo(t + 2, 1)

            with dve.Fori(0, T - 2) as t:
                step(t, True, True)
            step(T - 2, True, False)
            step(T - 1, False, False)
            for i in range(2):
                dve.wait_ge(co_full, i + 1)
                dve.tensor_tensor(c_out[:, 2 * i:2 * i + 2, :], work[i][:, :].rearrange("p (c n) -> p c n", c=2),
                                  shared.bo_row[:, :].unsqueeze(1).to_broadcast([P, 2, H]), ALU.add).then_inc(co_done, 1)
            dve.wait_ge(co_done, 2)
            dve.wait_ge(hp_done, 2 * T)

            def add_state(t):
                dve.tensor_tensor(hpre[:, t, 0, :], hpre[:, t, 0, :], c_out[:, 0, :], ALU.add).then_inc(dve_added, 1)

            def add_x(r, i, first):
                t = r * BACK + i
                dve.wait_ge(tanh_done, t + 1)
                dve.wait_ge(in_back[i], r * 16 + 16)
                if not first:
                    dve.wait_ge(stored[i], r * 16)
                dve.tensor_tensor(summed[:, i, :, :], x_back[:, i, :, :], hpre[:, t, :, :], ALU.add).then_inc(sum_done, 1)

            def round_of_steps(r, first, last):
                for i in range(BACK):
                    t = r * BACK + i
                    dve.wait_ge(sum_done, t + 1)
                    for c in range(TC):
                        dve.bn_stats(stats[:, i, c, :], summed[:, i, c, :]).then_inc(bn_done, 1)
                    if i + 1 < BACK:
                        add_x(r, i + 1, first)
                    elif not last:
                        add_x(r + 1, 0, False)
                    if i + LEAD < BACK or not last:
                        add_state(t + LEAD)
                    if not first:
                        dve.wait_ge(ln_step, t * 4 - (BACK - 1) * 4 + 3)
                    dve.wait_ge(bn_done, t * TC + TC)
                    dve.memset(fence[:, :], 0.0)
                    for c in range(TC):
                        dve.bn_aggr(mv[:, i, c, :], stats[:, i, c, :]).then_inc(mv_done, 1)

            for t in range(LEAD):
                add_state(t)
            add_x(0, 0, True)
            rounds(dve, round_of_steps)

        @block.tensor
        def _(pe):
            parts = [(0, 0), (1, 0), (0, 1)]

            def transpose_step(t, first):
                pe.wait_ge(x_in, t * 16 + 16)
                for k in range(KC):
                    if not first:
                        pe.wait_ge(hp_done, t * 2)
                    for c in range(TC):
                        last = pe.transpose(work[k][:, P * c:P * c + P], x_step[:, c, P * k:P * k + P], id_sb[:, :])
                    last.then_inc(xs_full, 1)

            def tokens_by(i, lhs, w, done):
                for j in range(2):
                    c = 2 * i + j
                    terms = [(k, a, d) for k in range(KC) for a, d in parts]
                    for m, (k, a, d) in enumerate(terms):
                        last = pe.matmul(work[i][:, H * j:H * j + H], lhs[a][:, k, P * c:P * c + P], (wo_h, wo_l)[d][:, w, k, :],
                                         start=(m == 0), stop=(m == len(terms) - 1))
                last.then_inc(done, 1)

            def gates_of(n, k, lhs, rhs, start, stop):
                g, mc = n % GATES, n // GATES
                for m, (a, d) in enumerate(parts):
                    last = pe.matmul(gate_ps[n][:, :], lhs[a][:, g, k, P * mc:P * mc + P], rhs[d][:, k, :],
                                     start=start and m == 0, stop=stop and m == len(parts) - 1)
                return last

            def from_x(t, first):
                pe.wait_ge(xs_lo, t * 2 + 2)
                if first:
                    pe.wait_ge(w_lo, 1)
                for i in range(2):
                    tokens_by(i, (xt_h, xt_l), 0, hp_full)
                if first:
                    pe.wait_ge(w_lo, 2)
                for n in range(GATES * KC):
                    if not first:
                        pe.wait_ge(gate_done, t * 6 - 5 + n)
                    for k in range(KC):
                        gates_of(n, k, (wx_h, wx_l), (xt_h, xt_l), k == 0, False)

            def from_state(t):
                for k in range(KC):
                    pe.wait_ge(s_lo, t * 2 + k + 1)
                    for n in range(GATES * KC):
                        last = gates_of(n, k, (uc_h, uc_l), (s_h, s_l), False, k == KC - 1)
                        if k == KC - 1:
                            last.then_inc(gate_full, 1)

            transpose_step(0, True)
            from_x(0, True)
            transpose_step(1, False)
            pe.wait_ge(w_lo, 3)
            with pe.Fori(0, T - 2) as t:
                from_state(t)
                from_x(t + 1, False)
                transpose_step(t + 2, False)
            from_state(T - 2)
            from_x(T - 1, False)
            from_state(T - 1)
            pe.wait_ge(s_lo, 2 * T + 2)
            pe.wait_ge(hp_done, 2 * T)
            pe.wait_ge(w_lo, 4)
            for i in range(2):
                tokens_by(i, (s_h, s_l), 1, co_full)


def build(nc, x, Wq, Wkv_short, Wkv_long, Wo, mix, decay, wx, uc, gate_bias, wo, uo, bo, in_c,
          ident, absdiff, qrows, krows, kab, out):
    x1 = nc.dram_tensor("x1_dram", [B, L, H], F32, kind="Internal").ap()
    with ExitStack() as ctx:
        shared = Shared(nc, ctx)
        attention_phase(nc, shared, x, x1, Wq, Wkv_short, Wkv_long, Wo, mix, decay, wx, uc, gate_bias, wo, uo, bo, in_c,
                        ident, absdiff, qrows, krows, kab)
        recurrence_phase(nc, shared, x1, out)


def constants():
    import numpy as np

    pos = np.arange(L, dtype=np.float32)
    chunk = np.arange(L) // P
    rows = ROWS - BIAS_ROW
    q = np.zeros((rows, 2, L), np.float32)
    k = np.zeros((rows, L), np.float32)
    kab = np.zeros((rows, 4), np.float32)
    for c in range(TC):
        sign, own = np.sign(chunk - c).astype(np.float32), (chunk == c).astype(np.float32)
        q[4 * c], q[4 * c + 1], q[4 * c + 2], q[4 * c + 3] = (t for t in (sign * pos, sign * pos, sign, sign))
        q[4 * c:4 * c + 4, 1] = 0
        k[4 * c:4 * c + 2], k[4 * c + 2:4 * c + 4] = -own, own * pos
    kab[:4 * TC, 0] = 1
    kab[4 * TC:, 1] = 1
    kab[1:4 * TC:2, 2] = -1
    q[MAX_ROW - BIAS_ROW, 1] = 1
    k[MAX_ROW - BIAS_ROW + 1] = 1
    q[MAX_ROW - BIAS_ROW:, 0] = 0
    return {"ident": np.eye(P, dtype=np.float32), "absdiff": np.abs(np.arange(P)[:, None] - np.arange(P)).astype(np.float32),
            "qrows": q.reshape(rows, 2 * L), "krows": k, "kab": kab}


def kernel(**inputs):
    import numpy as np
    import concourse.bacc as bacc
    from concourse.bass_utils import run_bass_kernel_spmd

    own = {k.removeprefix("L0_"): np.asarray(v) for k, v in inputs.items()}
    by_partition = lambda a: np.moveaxis(a.reshape(*a.shape[:-1], KC, P), -1, 0)
    t = lambda n: np.ascontiguousarray(own[n].T)
    arrays = {
        "x": own["attn_x"], "Wq": own["attn_Wq"], "Wkv_short": own["attn_Wkv_short"], "Wkv_long": own["attn_Wkv_long"],
        "Wo": own["attn_Wo"], "mix": own["attn_mix_weight"].reshape(1), "decay": own["attn_decay_factor"].reshape(1),
        "wx": np.stack([t("ffn_wf"), t("ffn_wi"), t("ffn_wc")]), "uc": np.stack([t("ffn_uf"), t("ffn_ui"), t("ffn_uc")]),
        "gate_bias": by_partition(np.stack([own["ffn_bf"], own["ffn_bi"], own["ffn_bc"]])),
        "wo": t("ffn_wo"), "uo": t("ffn_uo"), "bo": own["ffn_bo"], "in_c": by_partition(own["ffn_in_c"]),
    } | constants()
    arrays = {f"in_{k}": np.ascontiguousarray(v) for k, v in arrays.items()}
    nc = bacc.Bacc("TRN2", target_bir_lowering=False, num_devices=1)
    args = [nc.dram_tensor(k, v.shape, mybir.dt.from_np(v.dtype), kind="ExternalInput").ap() for k, v in arrays.items()]
    out = nc.dram_tensor("out", (B, L, H), F32, kind="ExternalOutput").ap()
    build(nc, *args, out)
    result = run_bass_kernel_spmd(nc, [arrays], core_ids=[0])
    return result.results[0]["out"]
```
